# Optimizing a Trainium2 kernel written in Bass

```python
import numpy as np
import jax
import jax.numpy as jnp

def _softmax(x, axis=-1):
    return jax.nn.softmax(x, axis=axis)

def _gelu(x):
    return jax.nn.gelu(x, approximate=True)

def _silu(x):
    return jax.nn.silu(x)

def _sigmoid(x):
    return jax.nn.sigmoid(x)

def _layernorm(x, axis=-1, eps=1e-05):
    m = jnp.mean(x, axis=axis, keepdims=True)
    v = jnp.var(x, axis=axis, keepdims=True)
    return (x - m) / jnp.sqrt(v + eps)

def _scatter_add(tgt, idx, src, axis=0):
    return tgt.at[idx].add(src)

def _segment_sum(src, seg, n):
    return jax.ops.segment_sum(src, seg, n)
kernel_name = 'mk_adj_resnorm_d4_adj_r2_85d72c'

def setup_inputs(seed: int=0):
    np.random.seed(seed)
    _w = jnp.asarray

    def _rec_inputs():
        import jax
        import jax.numpy as jnp
        _gk = jax.random.key(seed)
        x = -0.0005207 + 1.001 * jax.random.normal(jax.random.fold_in(_gk, 1), (8, 1024, 128), jnp.float32)
        _a = jax.random.bernoulli(jax.random.fold_in(_gk, 2), 0.00195312, (1024, 1024))
        _a = jnp.logical_or(_a, jnp.swapaxes(_a, -1, -2))
        _a = jnp.logical_or(_a, jnp.eye(1024, dtype=bool))
        _af = _a.astype(jnp.float32)
        _af = _af * jax.random.uniform(jax.random.fold_in(_gk, 3), (1024, 1024), jnp.float32, 0.05, 5.22011)
        adj = _af
        return (x, adj)
    x, adj = _rec_inputs()

    def _L0_gnn_setup():
        import jax, jax.numpy as jnp
        import numpy as np
        B, N, D, OUT = (8, 1024, 128, 128)
        key = jax.random.key(seed)
        k1, k2, k3, k4, k5, k6 = jax.random.split(key, 6)
        stdv = 1.0 / np.sqrt(OUT)
        inputs = jax.random.normal(k1, (B, N, D), dtype=jnp.float32)
        relation = jax.random.normal(k2, (N, N), dtype=jnp.float32)
        gl = 1.0 / np.sqrt(2 * D + 1)
        g_w = jax.random.uniform(k3, (2 * D + 1,), minval=-gl, maxval=gl, dtype=jnp.float32)
        g_b = jax.random.uniform(k4, (), minval=-gl, maxval=gl, dtype=jnp.float32)
        weight = jax.random.uniform(k5, (D, OUT), minval=-stdv, maxval=stdv, dtype=jnp.float32)
        bias = jax.random.uniform(k6, (OUT,), minval=-stdv, maxval=stdv, dtype=jnp.float32)
        return {'inputs': inputs, 'relation': relation, 'g_w': g_w, 'g_b': g_b, 'weight': weight, 'bias': bias}
    _L0_gnn_all = _L0_gnn_setup()
    _L0_gnn_in = {k: v for k, v in _L0_gnn_all.items() if k in ('g_w', 'g_b', 'weight', 'bias')}
    del _L0_gnn_all

    def _L1_gnn_setup():
        import jax, jax.numpy as jnp
        import numpy as np
        B, N, F_IN, F_OUT = (4, 2048, 128, 128)
        NEG_SLOPE = 0.2
        EDGE_PROB = 0.05
        key = jax.random.key(seed)
        kx, ka, kw, ks, kd = jax.random.split(key, 5)
        x = jax.random.normal(kx, (B, N, F_IN), dtype=jnp.float32)
        a = (jax.random.uniform(ka, (N, N)) < EDGE_PROB).astype(jnp.float32)
        a = a.at[jnp.arange(N), jnp.arange(N)].set(1.0)
        bw = float(np.sqrt(6.0 / (F_IN + F_OUT)))
        w = jax.random.uniform(kw, (F_IN, F_OUT), minval=-bw, maxval=bw, dtype=jnp.float32)
        ba = float(np.sqrt(6.0 / (1 + F_OUT)))
        a_src = jax.random.uniform(ks, (F_OUT,), minval=-ba, maxval=ba, dtype=jnp.float32)
        a_dst = jax.random.uniform(kd, (F_OUT,), minval=-ba, maxval=ba, dtype=jnp.float32)
        return {'x': x, 'a': a, 'w': w, 'a_src': a_src, 'a_dst': a_dst}
    _L1_gnn_all = _L1_gnn_setup()
    _L1_gnn_in = {k: v for k, v in _L1_gnn_all.items() if k in ('w', 'a_src', 'a_dst')}
    del _L1_gnn_all

    def _L2_gnn_setup():
        import jax, jax.numpy as jnp
        import numpy as np
        B, N, F_IN, F_OUT, ORDERS = (32, 1024, 128, 128, 2)
        NUM_MATRICES = 2 * ORDERS + 1

        def _cheb_hops(x0, A, orders):
            hops = []
            x1 = jnp.einsum('bnf,nw->bwf', x0, A)
            hops.append(x1)
            xk_1, xk_2 = (x1, x0)
            for _ in range(2, orders + 1):
                x2 = 2.0 * jnp.einsum('bnf,nw->bwf', xk_1, A) - xk_2
                hops.append(x2)
                xk_1, xk_2 = (x2, xk_1)
            return hops
        key = jax.random.key(seed)
        k1, k2, k3, k4, k5 = jax.random.split(key, 5)
        X = jax.random.normal(k1, (B, N, F_IN), dtype=jnp.float32)
        A1 = jax.random.uniform(k2, (N, N), dtype=jnp.float32) * (2.0 / N)
        A2 = jax.random.uniform(k3, (N, N), dtype=jnp.float32) * (2.0 / N)
        stdv = 1.0 / np.sqrt(F_OUT)
        Theta1 = jax.random.uniform(k4, (F_IN * NUM_MATRICES, F_OUT), dtype=jnp.float32, minval=-stdv, maxval=stdv)
        bias = jax.random.uniform(k5, (F_OUT,), dtype=jnp.float32, minval=-stdv, maxval=stdv)
        return {'X': X, 'A1': A1, 'A2': A2, 'Theta1': Theta1, 'bias': bias}
    _L2_gnn_all = _L2_gnn_setup()
    _L2_gnn_in = {k: v for k, v in _L2_gnn_all.items() if k in ('Theta1', 'bias')}
    del _L2_gnn_all

    def _L3_gnn_setup():
        import jax, jax.numpy as jnp
        import numpy as np
        from jax import lax
        CONV_ORDER = 3

        def _chebyshev(adj, x, order):

            def step(carry, _):
                nxt = jnp.einsum('ij,bjc->bic', adj, carry)
                return (nxt, nxt)
            _, xs = lax.scan(step, x, None, length=order)
            return jnp.moveaxis(xs, 0, -1)
        key = jax.random.key(seed)
        k1, k2, k3, k4 = jax.random.split(key, 4)
        B, E, C_in, C_out, K, n_adjs = (8, 2048, 128, 128, CONV_ORDER, 2)
        x_1 = jax.random.normal(k1, (B, E, C_in), dtype=jnp.float32)
        adj0 = jax.random.normal(k2, (E, E), dtype=jnp.float32) / np.sqrt(E)
        adj1 = jax.random.normal(k3, (E, E), dtype=jnp.float32) / np.sqrt(E)
        kdim = K * n_adjs + 1
        std = 1.414 * np.sqrt(2.0 / float((C_in + C_out) * kdim))
        weight_1 = std * jax.random.normal(k4, (C_in, C_out, kdim), dtype=jnp.float32)
        return {'x_1': x_1, 'adj0': adj0, 'adj1': adj1, 'weight_1': weight_1}
    _L3_gnn_all = _L3_gnn_setup()
    _L3_gnn_in = {k: v for k, v in _L3_gnn_all.items() if k in ('weight_1',)}
    del _L3_gnn_all
    return {'x': x, 'adj': adj, 'L0_gnn_g_w': _L0_gnn_in['g_w'], 'L0_gnn_g_b': _L0_gnn_in['g_b'], 'L0_gnn_weight': _L0_gnn_in['weight'], 'L0_gnn_bias': _L0_gnn_in['bias'], 'L1_gnn_w': _L1_gnn_in['w'], 'L1_gnn_a_src': _L1_gnn_in['a_src'], 'L1_gnn_a_dst': _L1_gnn_in['a_dst'], 'L2_gnn_Theta1': _L2_gnn_in['Theta1'], 'L2_gnn_bias': _L2_gnn_in['bias'], 'L3_gnn_weight_1': _L3_gnn_in['weight_1']}

def reference(x, adj, L0_gnn_g_w, L0_gnn_g_b, L0_gnn_weight, L0_gnn_bias, L1_gnn_w, L1_gnn_a_src, L1_gnn_a_dst, L2_gnn_Theta1, L2_gnn_bias, L3_gnn_weight_1):
    import jax
    import jax.numpy as jnp

    def _L0_gnn_ref(inputs, relation, g_w, g_b, weight, bias):
        import jax, jax.numpy as jnp
        import numpy as np
        B, N, D, OUT = (8, 1024, 128, 128)
        b, n, d = inputs.shape
        w_j = g_w[:d]
        w_i = g_w[d:2 * d]
        w_r = g_w[2 * d]
        sj = inputs @ w_j
        si = inputs @ w_i
        res = si[:, :, None] + sj[:, None, :] + relation[None] * w_r + g_b
        agg = jnp.einsum('bij,bjd->bid', res, inputs)
        return agg @ weight + bias

    def _L1_gnn_ref(x, a, w, a_src, a_dst):
        import jax, jax.numpy as jnp
        import numpy as np
        B, N, F_IN, F_OUT = (4, 2048, 128, 128)
        NEG_SLOPE = 0.2
        EDGE_PROB = 0.05
        h = jnp.einsum('bnf,fo->bno', x, w)
        e_src = jnp.einsum('bno,o->bn', h, a_src)
        e_dst = jnp.einsum('bno,o->bn', h, a_dst)
        e = jax.nn.leaky_relu(e_src[:, :, None] + e_dst[:, None, :], negative_slope=NEG_SLOPE)
        mask = (a > 0)[None, :, :]
        e = jnp.where(mask, e, -jnp.inf)
        alpha = jax.nn.softmax(e, axis=-1)
        out = jnp.einsum('bij,bjo->bio', alpha, h)
        return out

    def _L2_gnn_ref(X, A1, A2, Theta1, bias):
        import jax, jax.numpy as jnp
        import numpy as np
        B, N, F_IN, F_OUT, ORDERS = (32, 1024, 128, 128, 2)
        NUM_MATRICES = 2 * ORDERS + 1

        def _cheb_hops(x0, A, orders):
            hops = []
            x1 = jnp.einsum('bnf,nw->bwf', x0, A)
            hops.append(x1)
            xk_1, xk_2 = (x1, x0)
            for _ in range(2, orders + 1):
                x2 = 2.0 * jnp.einsum('bnf,nw->bwf', xk_1, A) - xk_2
                hops.append(x2)
                xk_1, xk_2 = (x2, xk_1)
            return hops
        xs = [X] + _cheb_hops(X, A1, ORDERS) + _cheb_hops(X, A2, ORDERS)
        x = jnp.stack(xs, axis=2)
        b, n = (X.shape[0], X.shape[1])
        x = x.reshape(b, n, -1)
        out = jax.nn.relu(x @ Theta1 + bias)
        return out

    def _L3_gnn_ref(x_1, adj0, adj1, weight_1):
        import jax, jax.numpy as jnp
        import numpy as np
        from jax import lax
        CONV_ORDER = 3

        def _chebyshev(adj, x, order):

            def step(carry, _):
                nxt = jnp.einsum('ij,bjc->bic', adj, carry)
                return (nxt, nxt)
            _, xs = lax.scan(step, x, None, length=order)
            return jnp.moveaxis(xs, 0, -1)
        parts = [x_1[..., None], _chebyshev(adj0, x_1, CONV_ORDER), _chebyshev(adj1, x_1, CONV_ORDER)]
        x_all = jnp.concatenate(parts, axis=3)
        y_1 = jnp.einsum('bnik,iok->bno', x_all, weight_1)
        return y_1
    x = _layernorm(x + _L0_gnn_ref(x, adj, L0_gnn_g_w, L0_gnn_g_b, L0_gnn_weight, L0_gnn_bias), axis=-1)
    x = _layernorm(x + _L1_gnn_ref(x, adj, L1_gnn_w, L1_gnn_a_src, L1_gnn_a_dst), axis=-1)
    x = _layernorm(x + _L2_gnn_ref(x, adj, adj, L2_gnn_Theta1, L2_gnn_bias), axis=-1)
    x = _layernorm(x + _L3_gnn_ref(x, adj, adj, L3_gnn_weight_1), axis=-1)
    return x

_drawn_inputs = setup_inputs


def setup_inputs(seed=0):
    import zlib

    import numpy as np

    out = dict(_drawn_inputs(seed))
    spreads = {}
    factors = {'L0_gnn_bias': 8.0, 'L1_gnn_a_src': 64.0, 'L1_gnn_a_dst': 4.391, 'L2_gnn_bias': 22.107}
    for name, (base, spread) in spreads.items():
        noise = np.random.default_rng([zlib.crc32(name.encode()), seed]).standard_normal(out[name].shape)
        drawn = base * np.exp(spread * noise) if base else spread * noise
        out[name] = jnp.asarray(drawn.astype(out[name].dtype))
    for name, factor in factors.items():
        out[name] = (out[name] * factor).astype(out[name].dtype)
    return out
```

```python
from contextlib import ExitStack

import concourse.bass as bass
from concourse import mybir

ALU = mybir.AluOpType
ACT = mybir.ActivationFunctionType
F32 = mybir.dt.float32
F32R = mybir.dt.float32r
BF16 = mybir.dt.bfloat16

P = 128
S = 2
EPS = 1e-5
SLOPE = 0.2
FAR = -1e30


def gnn_kernel(
    nc: bass.Bass,
    x: bass.AP,
    adj: bass.AP,
    g_w: bass.AP,
    g_b: bass.AP,
    w_rel: bass.AP,
    b_rel: bass.AP,
    w_att: bass.AP,
    a_src: bass.AP,
    a_dst: bass.AP,
    theta: bass.AP,
    b_cheb: bass.AP,
    w_conv: bass.AP,
    out: bass.AP,
):
    B, N, D = x.shape
    NB = N // P
    PAIRS = B // S
    K_CHEB = theta.shape[0] // D
    K_CONV = w_conv.shape[2]
    assert D == P and w_att.shape == (D, D) and K_CHEB == 5 and K_CONV == 7 and NB == 8

    x_v = x.rearrange("(q s) (ib p) d -> q s p ib d", s=S, p=P)
    out_v = out.rearrange("(q s) (ib p) d -> q s p ib d", s=S, p=P)
    adj_v = adj.rearrange("(nb p) w -> nb p w", p=P)

    mid = nc.dram_tensor("after_attention", (B, N, D), F32, kind="Internal").ap()
    mid_v = mid.rearrange("(q s) (ib p) d -> q s p ib d", s=S, p=P)
    dst_row = nc.dram_tensor("dst_row", (S, N), F32, kind="Internal").ap()
    shift_row = nc.dram_tensor("shift_row", (S, 2, N), F32, kind="Internal").ap()

    def wait(eng, sem, value):
        if not isinstance(value, int) or value > 0:
            eng.wait_ge(sem, value)

    ctx = ExitStack()
    with ctx:
        def sb(name, shape, dt=F32, c=ctx):
            return c.enter_context(nc.sbuf_tensor(name, shape, dt))

        def psum(name, shape, c=ctx):
            return c.enter_context(nc.psum_tensor(name, shape, F32))

        def sem(name, c=ctx):
            return c.enter_context(nc.semaphore(name))

        at_hi = sb("at_hi", [P, NB, N], F32R)
        at_lo = sb("at_lo", [P, NB, N], F32R)
        ident = sb("ident", [P, P])
        eps_t = sb("eps_t", [P, S * NB])
        half_t = sb("half_t", [P, S * NB])

        with ExitStack() as c12:
            ones = sb("ones", [P, P], F32, c12)
            mask_n = sb("mask_n", [P, NB, N], BF16, c12)
            mask_t = sb("mask_t", [P, NB, N], BF16, c12)
            w0 = sb("w0", [P, D + 2], F32, c12)
            w1 = sb("w1", [P, D + 2], F32, c12)
            w_r = sb("w_r", [P, 1], F32, c12)
            gb = sb("gb", [P, 1], F32, c12)
            bias0 = sb("bias0", [P, S, D], F32, c12)
            h_ext = sb("h_ext", [P, S, NB, D + 1], F32, c12)

            with ExitStack() as c:
                a_in = sb("a_in", [P, NB, N], F32, c)
                att_w_t = sb("att_w_t", [P, D], F32, c)
                a_sd = sb("a_sd", [P, 2], F32, c)
                tp = psum("tp", [P, 4, 512], c)
                tw = psum("tw", [P, 512], c)
                td = psum("td", [P, 512], c)
                adj_in = [sem(f"adj_in{n}", c) for n in range(NB)]
                w_in = sem("w_in", c)
                g_in = sem("g_in", c)
                att_in = sem("att_in", c)
                zeroed = sem("zeroed", c)
                made = sem("made", c)
                t_ready = sem("t_ready", c)
                hi_done = sem("hi_done", c)
                lo_done = sem("lo_done", c)
                wt_ready = sem("wt_ready", c)
                wt_done = sem("wt_done", c)
                wsd_ready = sem("wsd_ready", c)
                block = c.enter_context(nc.Block())

                @block.sync
                def _(sp):
                    for n in range(NB):
                        sp.dma_start(a_in[:, n, :], adj_v[n]).then_inc(adj_in[n], 16)
                    sp.dma_start(w0[:, 0:D], w_rel).then_inc(w_in, 16)
                    col = g_w.rearrange("(n a) -> n a", a=1)
                    sp.dma_start(w0[:, D:D + 1], col[D:2 * D, :]).then_inc(w_in, 16)
                    sp.dma_start(w0[:, D + 1:D + 2], col[0:D, :]).then_inc(w_in, 16)
                    sp.dma_start(w_r[:], g_w[2 * D:2 * D + 1].partition_broadcast(P)).then_inc(w_in, 16)
                    sp.dma_start(gb[:], g_b.rearrange("(a b) -> a b", a=1)[0].partition_broadcast(P)).then_inc(w_in, 16)
                    for s in range(S):
                        sp.dma_start(bias0[:, s, :], b_rel.partition_broadcast(P)).then_inc(w_in, 16)
                    sp.wait_ge(w_in, 16 * (5 + S))

                @block.gpsimd
                def _(pool):
                    pool.memset(ident[:], 0.0).then_inc(zeroed, 1)
                    pool.wait_ge(zeroed, 1)
                    pool.affine_select(out=ident[:], in_=ident[:], compare_op=ALU.not_equal, fill=1.0,
                                       base=0, pattern=[[-1, P]], channel_multiplier=1).then_inc(made, 1)
                    pool.memset(ones[:], 1.0)
                    pool.memset(eps_t[:], EPS)
                    pool.memset(half_t[:], -0.5)
                    pool.memset(h_ext[:, :, :, D:D + 1], 1.0)

                @block.tensor
                def _(pe):
                    pe.wait_ge(made, 1)
                    pe.wait_ge(att_in, 64)
                    nc.tensor.transpose(tw[:, 0:P], w1[:, 0:D], ident[:]).then_inc(wt_ready, 1)
                    for h in range(2):
                        for jb in range(NB):
                            u = h * NB + jb
                            if u >= 4:
                                pe.wait_ge(lo_done, u - 3)
                            for k in range(4):
                                ib = h * 4 + k
                                if jb == 0:
                                    pe.wait_ge(adj_in[ib], 16)
                                last = nc.tensor.transpose(tp[:, u % 4, k * P:(k + 1) * P],
                                                           a_in[:, ib, jb * P:(jb + 1) * P], ident[:])
                            last.then_inc(t_ready, 1)
                    pe.wait_ge(wt_done, 1)
                    nc.tensor.matmul(td[:, 0:2], att_w_t[:], a_sd[:], start=True, stop=True).then_inc(wsd_ready, 1)

                @block.scalar
                def _(act):
                    act.dma_start(w1[:, 0:D], w_att).then_inc(att_in, 16)
                    act.dma_start(a_sd[:, 0:1], a_src.rearrange("(n a) -> n a", a=1)).then_inc(att_in, 16)
                    act.dma_start(a_sd[:, 1:2], a_dst.rearrange("(n a) -> n a", a=1)).then_inc(att_in, 16)
                    act.dma_start(w1[:, D:D + 1], a_dst.rearrange("(n a) -> n a", a=1)).then_inc(att_in, 16)
                    act.wait_ge(wt_ready, 1)
                    nc.scalar.activation(att_w_t[:], tw[:, 0:P], ACT.Copy).then_inc(wt_done, 1)
                    for u in range(2 * NB):
                        h, jb = u // NB, u % NB
                        act.wait_ge(t_ready, u + 1)
                        nc.scalar.activation(at_hi[:, jb, h * 512:(h + 1) * 512], tp[:, u % 4, :],
                                             ACT.Copy).then_inc(hi_done, 1)
                    act.wait_ge(wsd_ready, 1)
                    nc.scalar.activation(w1[:, D:D + 2], td[:, 0:2], ACT.Copy)

                @block.vector
                def _(dve):
                    for n in range(NB):
                        dve.wait_ge(adj_in[n], 16)
                        nc.vector.tensor_scalar(mask_n[:, n, :], a_in[:, n, :], 0.0, FAR, ALU.is_le, ALU.mult)
                    for u in range(2 * NB):
                        h, jb = u // NB, u % NB
                        half = slice(h * 512, (h + 1) * 512)
                        dve.wait_ge(hi_done, u + 1)
                        nc.vector.tensor_scalar(mask_t[:, jb, half], tp[:, u % 4, :], 0.0, FAR,
                                                ALU.is_le, ALU.mult)
                        nc.vector.tensor_tensor(at_lo[:, jb, half], tp[:, u % 4, :],
                                                at_hi[:, jb, half].bitcast(F32), ALU.subtract).then_inc(lo_done, 1)

            with ExitStack() as c:
                TILES = 4
                x0 = sb("x0", [P, NB, S, D], F32, c)
                x1 = sb("x1", [P, S, NB, D], F32, c)
                x_t = sb("x_t", [P, S, N], F32, c)
                v_f = sb("v_f", [P, NB, S, D], F32, c)
                v_hi = sb("v_hi", [P, NB, S, D], F32R, c)
                v_lo = sb("v_lo", [P, NB, S, D], F32R, c)
                s_ij = sb("s_ij", [P, NB, S, 2], F32, c)
                s_ig = sb("s_ig", [P, NB, S, 1], F32, c)
                sums = sb("sums", [P, 2, S, D], F32, c)
                y_t = sb("y_t", [P, S, D], F32, c)
                stats = sb("stats", [P, S, NB, 6], F32, c)
                mv0 = sb("mv0", [P, S, NB, 2], F32, c)
                mv1 = sb("mv1", [P, NB, 2], F32, c)
                stats1 = sb("stats1", [P, NB, 6], F32, c)
                var_e = sb("var_e", [P, S, NB], F32, c)
                rs0 = sb("rs0", [P, S, NB], F32, c)
                rs1 = sb("rs1", [P, NB], F32, c)
                e_sd = sb("e_sd", [P, S, NB, 2], F32, c)
                e_d2 = sb("e_d2", [P, S, NB], F32, c)
                top = sb("top", [P, S, NB], F32, c)
                z_t = sb("z_t", [P, S, NB], F32, c)
                m_t = sb("m_t", [P, S, NB], F32, c)
                shift = sb("shift", [P, S, 2, NB], F32, c)
                dst_bc = sb("dst_bc", [P, S, N], F32, c)
                shift_bc = sb("shift_bc", [P, S, 2, N], F32, c)
                junk = sb("junk", [P, 2, N], BF16, c)
                pt = sb("pt", [P, TILES, N], F32, c)
                r_den = sb("r_den", [P, NB], F32, c)

                RING = 5
                ring = psum("ring", [P, RING, 512], c)
                att = psum("att", [P, 3, 512], c)
                GROUPS = [(0, 3), (3, 3), (6, 2)]

                kinds = ["a"] * 4 + ["d"] * 6 + ["d"] + ["d"] * NB + ["a"] * 5 + ["a"] * 5
                U_T, U_V, U_S, U_Y, U_H = 0, 4, 10, 11, 19
                UNITS = len(kinds)
                SLOTS = UNITS + 1
                assert SLOTS % RING == 0
                REL = {k: kinds.count(k) for k in "ad"}
                order = [kinds[:u + 1].count(kinds[u]) for u in range(UNITS)]

                x_in = [sem(f"x_in{s}", c) for s in range(S)]
                unit_ready = sem("unit_ready", c)
                freed = {"a": sem("freed_by_scalar", c), "d": sem("freed_by_vector", c)}
                v_hi_done = sem("v_hi_done", c)
                summed = sem("summed", c)
                mv0_ready = sem("mv0_ready", c)
                rs0_ready = sem("rs0_ready", c)
                x1_ready = [sem(f"x1_ready{s}", c) for s in range(S)]
                x1_copied = [sem(f"x1_copied{s}", c) for s in range(S)]
                dst_out = [sem(f"dst_out{s}", c) for s in range(S)]
                dst_in = [sem(f"dst_in{s}", c) for s in range(S)]
                shift_ready = [sem(f"shift_ready{s}", c) for s in range(S)]
                shift_out = [sem(f"shift_out{s}", c) for s in range(S)]
                shift_in = [sem(f"shift_in{s}", c) for s in range(S)]
                tile_free = sem("tile_free", c)
                w_ready = sem("w_ready", c)
                leaky_done = sem("leaky_done", c)
                masked = sem("masked", c)
                exp_done = sem("exp_done", c)
                att_free = sem("att_free", c)
                mv1_ready = sem("mv1_ready", c)
                rs1_ready = sem("rs1_ready", c)
                x2_ready = [sem(f"x2_ready{s}", c) for s in range(S)]
                stored = [sem(f"stored{s}", c) for s in range(S)]
                step = sem("step", c)
                pool_step = sem("pool_step", c)
                block = c.enter_context(nc.Block())

                def v_view(bank, n):
                    return ring[:, bank, 0:n * (D + 2)].rearrange("p (k c) -> p k c", c=D + 2)

                @block.sync
                def _(sp):
                    def load_x(p, s):
                        sp.dma_start(x0[:, :, s, :], x_v[p, s]).then_inc(x_in[s], 16)

                    def spread_dst(p, s):
                        sp.wait_ge(freed["a"], p * REL["a"] + order[U_H + 5 * s + 4])
                        sp.dma_start(dst_row[s].rearrange("(ib p) -> p ib", p=P), e_sd[:, s, :, 1],
                                     allow_slow_non_contiguous=True).then_inc(dst_out[s], 16)
                        sp.wait_ge(dst_out[s], p * 16 + 16)
                        sp.dma_start(dst_bc[:, s, :], dst_row[s].partition_broadcast(P)).then_inc(dst_in[s], 16)

                    def spread_shift(p, s):
                        sp.wait_ge(shift_ready[s], p + 1)
                        for k in range(2):
                            sp.dma_start(shift_row[s, k].rearrange("(ib p) -> p ib", p=P), shift[:, s, k, :],
                                         allow_slow_non_contiguous=True).then_inc(shift_out[s], 16)
                        sp.wait_ge(shift_out[s], p * 32 + 32)
                        for k in range(2):
                            sp.dma_start(shift_bc[:, s, k, :], shift_row[s, k].partition_broadcast(P)).then_inc(shift_in[s], 16)

                    def store(p, s):
                        sp.wait_ge(x2_ready[s], p + 1)
                        sp.dma_start(mid_v[p, s], x1[:, s, :, :]).then_inc(stored[s], 16)

                    def steady(p, more):
                        for s in range(S):
                            spread_shift(p, s)
                        for s in range(S):
                            store(p, s)
                            spread_dst(p + 1, s)
                            if more:
                                sp.wait_ge(x1_copied[s], p + 2)
                                load_x(p + 2, s)

                    for s in range(S):
                        load_x(0, s)
                    for s in range(S):
                        spread_dst(0, s)
                        sp.wait_ge(x1_copied[s], 1)
                        load_x(1, s)
                    with sp.Fori(0, PAIRS - 2) as p:
                        steady(p, True)
                    steady(PAIRS - 2, False)
                    for s in range(S):
                        spread_shift(PAIRS - 1, s)
                    for s in range(S):
                        store(PAIRS - 1, s)
                    for s in range(S):
                        sp.wait_ge(stored[s], 16 * PAIRS)

                @block.tensor
                def _(pe):
                    def bank(p, u):
                        before = u - RING
                        if before < 0:
                            before = before + SLOTS
                            p = p - 1
                        if before == UNITS:
                            before -= RING
                        if not (isinstance(p, int) and p < 0):
                            wait(pe, freed[kinds[before]], p * REL[kinds[before]] + order[before])
                        return u % RING

                    def transposes(p, u, s):
                        for half in range(2):
                            b = bank(p, u + half)
                            for k in range(4):
                                last = nc.tensor.transpose(ring[:, b, k * P:(k + 1) * P],
                                                           x0[:, half * 4 + k, s, :], ident[:])
                            last.then_inc(unit_ready, 1)

                    def project(p, u, u_t, s, w):
                        wait(pe, freed["a"], p * REL["a"] + order[u_t + 1])
                        for g, (b0, n) in enumerate(GROUPS):
                            b = bank(p, u + g)
                            for k in range(n):
                                last = nc.tensor.matmul(v_view(b, n)[:, k, :], x_t[:, s, (b0 + k) * P:(b0 + k + 1) * P],
                                                        w[:], start=True, stop=True)
                            last.then_inc(unit_ready, 1)

                    def relation(p):
                        for s in range(S):
                            pe.wait_ge(x_in[s], p * 16 + 16)
                            transposes(p, U_T + 2 * s, s)
                        for s in range(S):
                            project(p, U_V + 3 * s, U_T + 2 * s, s, w0)
                        b = bank(p, U_S)
                        wait(pe, freed["d"], p * REL["d"] + order[U_S - 1])
                        for jb in range(NB):
                            nc.tensor.matmul(ring[:, b, 0:S * D], ones[:], v_f[:, jb, :, :].rearrange("p s d -> p (s d)"),
                                             start=(jb == 0), stop=(jb == NB - 1))
                        for s in range(S):
                            for jb in range(NB):
                                last = nc.tensor.matmul(ring[:, b, (S + s) * D:(S + s + 1) * D],
                                                        s_ij[:, jb, s, 1:2].to_broadcast([P, P]), v_f[:, jb, s, :],
                                                        start=(jb == 0), stop=(jb == NB - 1))
                        last.then_inc(unit_ready, 1)
                        for ib in range(NB):
                            b = bank(p, U_Y + ib)
                            for jb in range(NB):
                                for n, (a, v) in enumerate(((at_hi, v_hi), (at_hi, v_lo), (at_lo, v_hi))):
                                    last = nc.tensor.matmul(ring[:, b, 0:S * D], a[:, jb, ib * P:(ib + 1) * P],
                                                            v[:, jb, :, :].rearrange("p s d -> p (s d)"),
                                                            start=(jb == 0 and n == 0), stop=(jb == NB - 1 and n == 2))
                            last.then_inc(unit_ready, 1)

                    def heads(p, s):
                        pe.wait_ge(x1_ready[s], p + 1)
                        transposes(p, U_H + 5 * s, s)
                        project(p, U_H + 5 * s + 2, U_H + 5 * s, s, w1)

                    def attend(p, s):
                        pe.wait_ge(att_free, p * S + (s + 1))
                        for jb in range(NB):
                            pe.wait_ge(exp_done, p * (S * NB) + (s * NB + jb + 1))
                            for g, (b0, n) in enumerate(GROUPS):
                                for k in range(n):
                                    last = nc.tensor.matmul(
                                        att[:, g, k * (D + 1):(k + 1) * (D + 1)],
                                        pt[:, jb % TILES, (b0 + k) * P:(b0 + k + 1) * P], h_ext[:, s, jb, :],
                                        start=(jb == 0 and k == 0), stop=(jb == NB - 1), skip_group_check=True)
                            last.then_inc(tile_free, 1)

                    pe.sem_inc(att_free, 1)
                    relation(0)
                    for s in range(S):
                        heads(0, s)
                    with pe.Fori(0, PAIRS - 1) as p:
                        relation(p + 1)
                        for s in range(S):
                            attend(p, s)
                            heads(p + 1, s)
                    for s in range(S):
                        attend(PAIRS - 1, s)

                @block.scalar
                def _(act):
                    def copy_t(p, u, s):
                        for half in range(2):
                            act.wait_ge(unit_ready, p * UNITS + (u + half + 1))
                            nc.scalar.activation(x_t[:, s, half * 512:(half + 1) * 512], ring[:, (u + half) % RING, :],
                                                 ACT.Copy).then_inc(freed["a"], 1)

                    def relation(p):
                        for s in range(S):
                            copy_t(p, U_T + 2 * s, s)
                        for s in range(S):
                            for g, (b0, n) in enumerate(GROUPS):
                                u = U_V + 3 * s + g
                                act.wait_ge(unit_ready, p * UNITS + (u + 1))
                                src = v_view(u % RING, n)[:, :, 0:D]
                                nc.scalar.activation(v_f[:, b0:b0 + n, s, :], src, ACT.Copy)
                                nc.scalar.activation(v_hi[:, b0:b0 + n, s, :], src, ACT.Copy,
                                                     scale=w_r[:, 0:1]).then_inc(v_hi_done, 1)

                    def heads(p, s):
                        u = U_H + 5 * s
                        copy_t(p, u, s)
                        for g, (b0, n) in enumerate(GROUPS):
                            act.wait_ge(unit_ready, p * UNITS + (u + 2 + g + 1))
                            src = v_view((u + 2 + g) % RING, n)
                            nc.scalar.activation(h_ext[:, s, b0:b0 + n, 0:D], src[:, :, 0:D], ACT.Copy)
                            nc.scalar.activation(e_sd[:, s, b0:b0 + n, :], src[:, :, D:D + 2],
                                                 ACT.Copy).then_inc(freed["a"], 1)
                        wait(act, stored[s], p * 16)
                        nc.scalar.activation(x1[:, s, :, :], x0[:, :, s, :], ACT.Copy).then_inc(x1_copied[s], 1)

                    def first(p, s, jb):
                        if jb == 0:
                            act.wait_ge(shift_in[s], p * 32 + 32)
                        act.wait_ge(tile_free, p * (S * NB) + (s * NB + jb + 1))
                        nc.scalar.activation(pt[:, jb % TILES, :], shift_bc[:, s, 0, :], ACT.Identity,
                                             bias=e_sd[:, s, jb, 1:2]).then_inc(w_ready, 1)

                    def expo(p, s, jb):
                        act.wait_ge(masked, p * (S * NB) + (s * NB + jb + 1))
                        nc.scalar.activation(pt[:, jb % TILES, :], pt[:, jb % TILES, :], ACT.Exp).then_inc(exp_done, 1)

                    def attend(p, s):
                        if s == 0:
                            for jb in range(TILES):
                                first(p, 0, jb)
                        for jb in range(NB):
                            expo(p, s, jb)
                            ahead = s * NB + jb + TILES
                            if ahead < S * NB:
                                first(p, ahead // NB, ahead % NB)

                    act.sem_inc(tile_free, TILES)
                    relation(0)
                    for s in range(S):
                        heads(0, s)
                    with act.Fori(0, PAIRS - 1) as p:
                        relation(p + 1)
                        for s in range(S):
                            attend(p, s)
                            heads(p + 1, s)
                    for s in range(S):
                        attend(PAIRS - 1, s)

                @block.vector
                def _(dve):
                    count = [0]

                    def link(ins):
                        count[0] += 1
                        ins.then_inc(step, 1)
                        dve.wait_ge(step, count[0])

                    def restart():
                        dve.sem_clear(step)
                        count[0] = 0

                    def project(p):
                        for s in range(S):
                            for g, (b0, n) in enumerate(GROUPS):
                                u = U_V + 3 * s + g
                                src = v_view(u % RING, n)
                                dve.wait_ge(v_hi_done, p * (2 * 3) + (s * 3 + g + 1))
                                for k in range(n):
                                    nc.vector.scalar_tensor_tensor(
                                        out=v_lo[:, b0 + k, s, :], in0=src[:, k, 0:D], scalar=w_r[:, 0:1],
                                        in1=v_hi[:, b0 + k, s, :].bitcast(F32), op0=ALU.mult, op1=ALU.subtract)
                                nc.vector.tensor_copy(s_ij[:, b0:b0 + n, s, :], src[:, :, D:D + 2]).then_inc(freed["d"], 1)
                        dve.wait_ge(freed["d"], p * REL["d"] + order[U_S - 1])
                        nc.vector.tensor_scalar(s_ig[:], s_ij[:, :, :, 0:1], gb[:, 0:1], None, ALU.add)
                        dve.wait_ge(unit_ready, p * UNITS + (U_S + 1))
                        src = ring[:, U_S % RING, :].rearrange("p (k s d) -> p k s d", k=2, s=S)
                        nc.vector.tensor_copy(sums[:, 0, :, :], src[:, 0, :, :])
                        nc.vector.tensor_tensor(sums[:, 1, :, :], src[:, 1, :, :], bias0[:], ALU.add).then_inc(freed["d"], 1)

                    def rows(p, b0, b1):
                        for ib in range(b0, b1):
                            u = U_Y + ib
                            dve.wait_ge(unit_ready, p * UNITS + (u + 1))
                            if ib == 0:
                                dve.wait_ge(summed, p * S + S)
                            for s in range(S):
                                last = nc.vector.scalar_tensor_tensor(
                                    out=y_t[:, s, :], in0=sums[:, 0, s, :], scalar=s_ig[:, ib, s, :],
                                    in1=ring[:, u % RING, s * D:(s + 1) * D], op0=ALU.mult, op1=ALU.add)
                            last.then_inc(freed["d"], 1)
                            dve.wait_ge(freed["d"], p * REL["d"] + order[u])
                            link(nc.vector.tensor_tensor(x0[:, ib, :, :], y_t[:], x0[:, ib, :, :], ALU.add))
                            for s in range(S):
                                last = nc.vector.bn_stats(stats[:, s, ib, :], x0[:, ib, s, :])
                            link(last)

                    def norm0(p):
                        for s in range(S):
                            for ib in range(NB):
                                last = nc.vector.bn_aggr(mv0[:, s, ib, :], stats[:, s, ib, :])
                            last.then_inc(mv0_ready, 1)
                        for s in range(S):
                            dve.wait_ge(rs0_ready, p * S + (s + 1))
                            for ib in range(NB):
                                last = nc.vector.tensor_scalar(x0[:, ib, s, :], x0[:, ib, s, :], mv0[:, s, ib, 0:1],
                                                               rs0[:, s, ib:ib + 1], ALU.subtract, ALU.mult)
                            last.then_inc(x1_ready[s], 1)

                    def maximum(p, s):
                        dve.wait_ge(dst_in[s], p * 16 + 16)
                        nc.vector.tensor_scalar(e_d2[:, s, :], e_sd[:, s, :, 1], SLOPE, None, ALU.mult)
                        for ib in range(NB):
                            link(nc.vector.tensor_tensor_reduce(junk[:, ib % 2, :], mask_n[:, ib, :], dst_bc[:, s, :], 1.0,
                                                                3 * FAR, ALU.add, ALU.max, top[:, s, ib:ib + 1]))
                        src = e_sd[:, s, :, 0]
                        link(nc.vector.tensor_tensor(z_t[:, s, :], src, top[:, s, :], ALU.add))
                        link(nc.vector.scalar_tensor_tensor(out=m_t[:, s, :], in0=z_t[:, s, :], scalar=SLOPE,
                                                            in1=z_t[:, s, :], op0=ALU.mult, op1=ALU.max))
                        nc.vector.tensor_tensor(shift[:, s, 0, :], src, m_t[:, s, :], ALU.subtract)
                        nc.vector.scalar_tensor_tensor(out=shift[:, s, 1, :], in0=src, scalar=SLOPE, in1=m_t[:, s, :],
                                                       op0=ALU.mult, op1=ALU.subtract).then_inc(shift_ready[s], 1)

                    def leaky(p, s):
                        for jb in range(NB):
                            dve.wait_ge(w_ready, p * (S * NB) + (s * NB + jb + 1))
                            tile = pt[:, jb % TILES, :]
                            nc.vector.scalar_tensor_tensor(out=tile, in0=shift_bc[:, s, 1, :], scalar=e_d2[:, s, jb:jb + 1],
                                                           in1=tile, op0=ALU.add, op1=ALU.max).then_inc(leaky_done, 1)

                    def finish(p, s):
                        dve.wait_ge(tile_free, p * (S * NB) + (s * NB + NB + TILES))
                        dve.wait_ge(x1_copied[s], p + 1)
                        for g, (b0, n) in enumerate(GROUPS):
                            src = att[:, g, 0:n * (D + 1)].rearrange("p (k c) -> p k c", c=D + 1)
                            last = nc.vector.reciprocal(r_den[:, b0:b0 + n], src[:, :, D])
                        link(last)
                        for g, (b0, n) in enumerate(GROUPS):
                            for k in range(n):
                                last = nc.vector.scalar_tensor_tensor(
                                    out=x1[:, s, b0 + k, :], in0=att[:, g, k * (D + 1):k * (D + 1) + D],
                                    scalar=r_den[:, b0 + k:b0 + k + 1], in1=x1[:, s, b0 + k, :], op0=ALU.mult, op1=ALU.add)
                        last.then_inc(att_free, 1)
                        dve.wait_ge(att_free, p * S + (s + 2))
                        for ib in range(NB):
                            last = nc.vector.bn_stats(stats1[:, ib, :], x1[:, s, ib, :])
                        link(last)
                        for ib in range(NB):
                            last = nc.vector.bn_aggr(mv1[:, ib, :], stats1[:, ib, :])
                        last.then_inc(mv1_ready, 1)
                        dve.wait_ge(rs1_ready, p * S + (s + 1))
                        for ib in range(NB):
                            last = nc.vector.tensor_scalar(x1[:, s, ib, :], x1[:, s, ib, :], mv1[:, ib, 0:1],
                                                           rs1[:, ib:ib + 1], ALU.subtract, ALU.mult)
                        last.then_inc(x2_ready[s], 1)

                    project(0)
                    rows(0, 0, NB)
                    norm0(0)
                    restart()
                    with dve.Fori(0, PAIRS - 1) as p:
                        project(p + 1)
                        maximum(p, 0)
                        rows(p + 1, 0, NB // 2)
                        maximum(p, 1)
                        rows(p + 1, NB // 2, NB)
                        norm0(p + 1)
                        for s in range(S):
                            leaky(p, s)
                            finish(p, s)
                        restart()
                    for s in range(S):
                        maximum(PAIRS - 1, s)
                    for s in range(S):
                        leaky(PAIRS - 1, s)
                        finish(PAIRS - 1, s)

                @block.gpsimd
                def _(pool):
                    def add_sums(p):
                        pool.wait_ge(freed["d"], p * REL["d"] + order[U_S])
                        for s in range(S):
                            row = sums[:, 1, s, :].unsqueeze(1).broadcast_to([P, NB, D])
                            pool.tensor_tensor(x0[:, :, s, :], x0[:, :, s, :], row, ALU.add).then_inc(summed, 1)

                    def root(mv, var_at, rs, ready, value, done):
                        pool.wait_ge(ready, value)
                        pool.tensor_tensor(var_at, mv, eps_t[:, 0:NB], ALU.add).then_inc(pool_step, 1)
                        pool.wait_ge(pool_step, 1)
                        pool.sem_clear(pool_step)
                        pool.tensor_tensor(rs, var_at, half_t[:, 0:NB], ALU.pow).then_inc(done, 1)

                    def relation(p):
                        add_sums(p)
                        for s in range(S):
                            root(mv0[:, s, :, 1], var_e[:, s, :], rs0[:, s, :], mv0_ready, p * S + (s + 1), rs0_ready)

                    def attend(p, s):
                        for jb in range(NB):
                            pool.wait_ge(leaky_done, p * (S * NB) + (s * NB + jb + 1))
                            tile = pt[:, jb % TILES, :]
                            pool.tensor_tensor(tile, tile, mask_t[:, jb, :], ALU.add).then_inc(masked, 1)
                        root(mv1[:, :, 1], var_e[:, s, :], rs1[:], mv1_ready, p * S + (s + 1), rs1_ready)

                    relation(0)
                    with pool.Fori(0, PAIRS - 1) as p:
                        relation(p + 1)
                        for s in range(S):
                            attend(p, s)
                    for s in range(S):
                        attend(PAIRS - 1, s)

        with ExitStack() as c:
            a_hi = sb("a_hi", [P, NB, N], F32R, c)
            a_lo = sb("a_lo", [P, NB, N], F32R, c)
            STAGE = 2
            a_in = sb("a_part", [P, STAGE, N], F32, c)
            xin = sb("xin", [P, NB, S, D], F32, c)
            xb = sb("xb", [P, NB, S, D], F32, c)
            x_t = sb("x_t3", [P, NB, S, D], F32, c)
            z_hi = sb("z_hi", [P, 2, NB, S, D], F32R, c)
            z_lo = sb("z_lo", [P, 2, NB, S, D], F32R, c)
            y_t = sb("y_t3", [P, S, D], F32, c)
            w_all = sb("w_all", [P, K_CONV * D], F32, c)
            w2 = sb("w2", [P, 3, D], F32, c)
            w3 = sb("w3", [P, 4, D], F32, c)
            bias2 = sb("bias2", [P, S, D], F32, c)
            stats = sb("stats3", [P, 2, S, 6], F32, c)
            mv = sb("mv3", [P, 2, S, 2], F32, c)
            var_e = sb("var_e3", [P, 2, S], F32, c)
            rs = sb("rs3", [P, 2, S], F32, c)
            RING = 8
            ring = psum("ring3", [P, RING, 512], c)

            HOPS = (2, 3)
            kinds, base = [], []
            for hops in HOPS:
                base.append(len(kinds))
                kinds += ["a"] * (NB // 2) + ["d"] * (NB * (1 + hops))
            UNITS = len(kinds)
            assert UNITS % RING == 0
            REL = {k: kinds.count(k) for k in "ad"}
            order = [kinds[:u + 1].count(kinds[u]) for u in range(UNITS)]
            SPLITS = NB * sum(HOPS)

            adj_in = [sem(f"adj_part{n}", c) for n in range(STAGE)]
            a_hi_done = sem("a_hi_done", c)
            a_lo_done = sem("a_lo_done", c)
            theta_in = sem("theta_in", c)
            conv_in = sem("conv_in", c)
            w2_ready = sem("w2_ready", c)
            w3_ready = sem("w3_ready", c)
            bias_in = sem("bias_in", c)
            x_in = sem("xin_in", c)
            copied = sem("copied", c)
            unit_ready = sem("unit_ready3", c)
            freed = {"a": sem("freed_by_scalar3", c), "d": sem("freed_by_vector3", c)}
            split_hi = sem("split_hi", c)
            mv_ready = sem("mv_ready3", c)
            rs_ready = sem("rs_ready3", c)
            normed = sem("normed", c)
            stored = sem("stored3", c)
            step = sem("step3", c)
            pool_step = sem("pool_step3", c)
            block = c.enter_context(nc.Block())
            BLOCKS = len(HOPS) * NB

            @block.sync
            def _(sp):
                def load_x(q):
                    for s in range(S):
                        sp.dma_start(xin[:, :, s, :], mid_v[q, s]).then_inc(x_in, 16)

                def store(q):
                    sp.wait_ge(normed, q * BLOCKS + BLOCKS)
                    for s in range(S):
                        sp.dma_start(out_v[q, s], xb[:, :, s, :]).then_inc(stored, 16)

                load_x(0)
                for n in range(NB):
                    if n >= STAGE:
                        sp.wait_ge(a_lo_done, n - STAGE + 1)
                    sp.dma_start(a_in[:, n % STAGE, :], adj_v[n]).then_inc(adj_in[n % STAGE], 16)
                for s in range(S):
                    sp.dma_start(bias2[:, s, :], b_cheb.partition_broadcast(P)).then_inc(bias_in, 16)
                with sp.Fori(0, PAIRS - 1) as q:
                    sp.wait_ge(copied, q + 1)
                    load_x(q + 1)
                    store(q)
                store(PAIRS - 1)
                sp.wait_ge(stored, 16 * S * PAIRS)

            @block.tensor
            def _(pe):
                def bank(q, u):
                    before = u - RING
                    if before < 0:
                        before, q = before + UNITS, q - 1
                    if not (isinstance(q, int) and q < 0):
                        wait(pe, freed[kinds[before]], q * REL[kinds[before]] + order[before])
                    return u % RING

                def times_w(q, b, ib, w, start):
                    for s in range(S):
                        last = nc.tensor.matmul(ring[:, b, s * D:(s + 1) * D], x_t[:, ib, s, :], w,
                                                start=start, stop=(start or s == S - 1))
                    return last

                def layer(q, n, src, a_h, a_l, w):
                    u = base[n]

                    def transposes(t):
                        if n == 0 and t == 0:
                            pe.wait_ge(x_in, q * (16 * S) + 16 * S)
                        if n == 1:
                            pe.wait_ge(normed, q * BLOCKS + (2 * t + 2))
                        b = bank(q, u + t)
                        for k in range(2):
                            for s in range(S):
                                last = nc.tensor.transpose(ring[:, b, (k * S + s) * P:(k * S + s + 1) * P],
                                                           src[:, 2 * t + k, s, :], ident[:])
                        last.then_inc(unit_ready, 1)

                    for t in range(NB // 2):
                        transposes(t)
                    u += NB // 2
                    if isinstance(q, int) and q == 0:
                        pe.wait_ge((w2_ready, w3_ready)[n], 1)
                    for ib in range(NB):
                        if ib % 2 == 0:
                            wait(pe, freed["a"], q * REL["a"] + order[base[n] + ib // 2])
                        b = bank(q, u + ib)
                        times_w(q, b, ib, w[:, 0, :], True).then_inc(unit_ready, 1)
                    for hop in range(HOPS[n]):
                        if isinstance(q, int) and q == 0 and n == 0 and hop == 0:
                            pe.wait_ge(a_lo_done, NB)
                        u += NB
                        for ib in range(NB):
                            b = bank(q, u + ib)
                            for jb in range(NB):
                                if ib == 0:
                                    wait(pe, freed["d"], q * REL["d"] + order[u - NB + jb])
                                for k, (a, z) in enumerate(((a_h, z_hi), (a_h, z_lo), (a_l, z_hi))):
                                    nc.tensor.matmul(ring[:, b, 0:S * D], a[:, jb, ib * P:(ib + 1) * P],
                                                     z[:, hop % 2, jb, :, :].rearrange("p s d -> p (s d)"),
                                                     start=(jb == 0 and k == 0), stop=False)
                            times_w(q, b, ib, w[:, hop + 1, :], False).then_inc(unit_ready, 1)

                def pair(q):
                    layer(q, 0, xin, a_hi, a_lo, w2)
                    layer(q, 1, xb, at_hi, at_lo, w3)

                pair(0)
                with pe.Fori(1, PAIRS) as q:
                    pair(q)

            @block.scalar
            def _(act):
                def layer(q, n):
                    u = base[n]
                    for t in range(NB // 2):
                        act.wait_ge(unit_ready, q * UNITS + (u + t + 1))
                        nc.scalar.activation(x_t[:, 2 * t:2 * t + 2, :, :].rearrange("p k s d -> p (k s d)"),
                                             ring[:, (u + t) % RING, :], ACT.Copy).then_inc(freed["a"], 1)
                    u += NB // 2
                    for k in range(HOPS[n]):
                        for ib in range(NB):
                            act.wait_ge(unit_ready, q * UNITS + (u + ib + 1))
                            nc.scalar.activation(z_hi[:, k % 2, ib, :, :].rearrange("p s d -> p (s d)"),
                                                 ring[:, (u + ib) % RING, 0:S * D], ACT.Copy).then_inc(split_hi, 1)
                        u += NB
                        if n == 0 and k == 0:
                            wait(act, stored, q * (16 * S))
                            nc.scalar.activation(xb[:], xin[:], ACT.Copy).then_inc(copied, 1)

                def pair(q):
                    layer(q, 0)
                    layer(q, 1)

                act.dma_start(w_all[:, 0:K_CHEB * D].rearrange("p (k o) -> p k o", o=D),
                              theta.rearrange("(k f) o -> f k o", f=D)).then_inc(theta_in, 16)
                act.wait_ge(w2_ready, 1)
                act.dma_start(w_all[:], w_conv.rearrange("i o k -> i (o k)")).then_inc(conv_in, 16)
                for n in range(NB):
                    act.wait_ge(adj_in[n % STAGE], 16 * (n // STAGE + 1))
                    nc.scalar.activation(a_hi[:, n, :], a_in[:, n % STAGE, :], ACT.Copy).then_inc(a_hi_done, 1)
                pair(0)
                with act.Fori(1, PAIRS) as q:
                    pair(q)

            @block.vector
            def _(dve):
                count = [0]

                def link(ins):
                    count[0] += 1
                    ins.then_inc(step, 1)
                    dve.wait_ge(step, count[0])

                def weights():
                    dve.wait_ge(theta_in, 16)
                    th = w_all[:, 0:K_CHEB * D].rearrange("p (k o) -> p k o", o=D)
                    nc.vector.tensor_tensor(w2[:, 1, :], th[:, 1, :], th[:, 3, :], ALU.add)
                    link(nc.vector.tensor_tensor(w2[:, 0, :], th[:, 2, :], th[:, 4, :], ALU.add))
                    link(nc.vector.tensor_tensor(w2[:, 2, :], th[:, 0, :], w2[:, 0, :], ALU.subtract))
                    nc.vector.tensor_scalar(w2[:, 0, :], w2[:, 0, :], 2.0, None, ALU.mult).then_inc(w2_ready, 1)
                    dve.wait_ge(conv_in, 16)
                    cv = w_all[:].rearrange("p (o k) -> p k o", k=K_CONV)
                    nc.vector.tensor_copy(w3[:, 3, :], cv[:, 0, :])
                    for k in range(3):
                        last = nc.vector.tensor_tensor(w3[:, 2 - k, :], cv[:, 1 + k, :], cv[:, 4 + k, :], ALU.add)
                    last.then_inc(w3_ready, 1)

                def stats_of(ib):
                    for s in range(S):
                        last = nc.vector.bn_stats(stats[:, ib % 2, s, :], xb[:, ib, s, :])
                    link(last)
                    for s in range(S):
                        last = nc.vector.bn_aggr(mv[:, ib % 2, s, :], stats[:, ib % 2, s, :])
                    last.then_inc(mv_ready, 1)

                def norm(q, n, ib):
                    dve.wait_ge(rs_ready, q * BLOCKS + (n * NB + ib + 1))
                    for s in range(S):
                        last = nc.vector.tensor_scalar(xb[:, ib, s, :], xb[:, ib, s, :], mv[:, ib % 2, s, 0:1],
                                                       rs[:, ib % 2, s:s + 1], ALU.subtract, ALU.mult)
                    last.then_inc(normed, 1)

                def layer(q, n):
                    u = base[n] + NB // 2
                    done = NB * sum(HOPS[:n])
                    for k in range(HOPS[n]):
                        for ib in range(NB):
                            dve.wait_ge(split_hi, q * SPLITS + (done + k * NB + ib + 1))
                            nc.vector.tensor_tensor(z_lo[:, k % 2, ib, :, :].rearrange("p s d -> p (s d)"),
                                                    ring[:, (u + ib) % RING, 0:S * D],
                                                    z_hi[:, k % 2, ib, :, :].rearrange("p s d -> p (s d)").bitcast(F32),
                                                    ALU.subtract).then_inc(freed["d"], 1)
                        u += NB
                    for ib in range(NB):
                        if n == 0 and ib == 0:
                            dve.wait_ge(copied, q + 1)
                        dve.wait_ge(unit_ready, q * UNITS + (u + ib + 1))
                        got = ring[:, (u + ib) % RING, 0:S * D].rearrange("p (s d) -> p s d", s=S)
                        if n == 0:
                            nc.vector.tensor_tensor(y_t[:], got, bias2[:], ALU.add).then_inc(freed["d"], 1)
                            dve.wait_ge(freed["d"], q * REL["d"] + order[u + ib])
                            link(nc.vector.scalar_tensor_tensor(out=xb[:, ib, :, :].rearrange("p s d -> p (s d)"),
                                                                in0=y_t[:].rearrange("p s d -> p (s d)"), scalar=0.0,
                                                                in1=xb[:, ib, :, :].rearrange("p s d -> p (s d)"),
                                                                op0=ALU.max, op1=ALU.add))
                        else:
                            nc.vector.tensor_tensor(xb[:, ib, :, :], got, xb[:, ib, :, :], ALU.add).then_inc(freed["d"], 1)
                            dve.wait_ge(freed["d"], q * REL["d"] + order[u + ib])
                        stats_of(ib)
                        if ib > 0:
                            norm(q, n, ib - 1)
                    norm(q, n, NB - 1)

                def pair(q):
                    layer(q, 0)
                    layer(q, 1)
                    dve.sem_clear(step)
                    count[0] = 0

                weights()
                for n in range(NB):
                    dve.wait_ge(a_hi_done, n + 1)
                    nc.vector.tensor_tensor(a_lo[:, n, :], a_in[:, n % STAGE, :], a_hi[:, n, :].bitcast(F32),
                                            ALU.subtract).then_inc(a_lo_done, 1)
                dve.wait_ge(bias_in, 16 * S)
                pair(0)
                with dve.Fori(1, PAIRS) as q:
                    pair(q)

            @block.gpsimd
            def _(pool):
                def roots(q):
                    for n in range(BLOCKS):
                        k = n % 2
                        pool.wait_ge(mv_ready, q * BLOCKS + (n + 1))
                        pool.tensor_tensor(var_e[:, k, :], mv[:, k, :, 1], eps_t[:, 0:S], ALU.add).then_inc(pool_step, 1)
                        pool.wait_ge(pool_step, 1)
                        pool.sem_clear(pool_step)
                        pool.tensor_tensor(rs[:, k, :], var_e[:, k, :], half_t[:, 0:S], ALU.pow).then_inc(rs_ready, 1)

                with pool.Fori(0, PAIRS) as q:
                    roots(q)


_INS = ['x', 'adj', 'L0_gnn_g_w', 'L0_gnn_g_b', 'L0_gnn_weight', 'L0_gnn_bias', 'L1_gnn_w', 'L1_gnn_a_src',
        'L1_gnn_a_dst', 'L2_gnn_Theta1', 'L2_gnn_bias', 'L3_gnn_weight_1']
_OUTS = [((8, 1024, 128), 'float32')]


def kernel(**inputs):
    import numpy as _np
    import concourse.bacc as _bacc
    from concourse import mybir as _mybir
    from concourse.bass_utils import run_bass_kernel_spmd as _run

    nc = _bacc.Bacc("TRN2", target_bir_lowering=False, num_devices=1)
    arrays, args = {}, []
    for name in _INS:
        a = _np.ascontiguousarray(inputs[name]).reshape(_np.shape(inputs[name]) or (1,))
        arrays[f"in_{name}_dram"] = a
        args.append(nc.dram_tensor(f"in_{name}_dram", a.shape, _mybir.dt.from_np(a.dtype), kind="ExternalInput").ap())
    for i, (shape, dtype) in enumerate(_OUTS):
        dt = _mybir.dt.from_np(_np.dtype(dtype))
        args.append(nc.dram_tensor(f"out_{i}_dram", shape, dt, kind="ExternalOutput").ap())
    gnn_kernel(nc, *args)
    r = _run(nc, [arrays], core_ids=[0])
    got = tuple(r.results[0][f"out_{i}_dram"] for i in range(len(_OUTS)))
    return got[0]
```

```python
from contextlib import ExitStack

import concourse.bass as bass
from concourse import mybir

ALU = mybir.AluOpType
ACT = mybir.ActivationFunctionType
F32 = mybir.dt.float32
F32R = mybir.dt.float32r
BF16 = mybir.dt.bfloat16

P = 128
S = 2
EPS = 1e-5
SLOPE = 0.2
FAR = -1e30


def gnn_kernel(
    nc: bass.Bass,
    x: bass.AP,
    adj: bass.AP,
    g_w: bass.AP,
    g_b: bass.AP,
    w_rel: bass.AP,
    b_rel: bass.AP,
    w_att: bass.AP,
    a_src: bass.AP,
    a_dst: bass.AP,
    theta: bass.AP,
    b_cheb: bass.AP,
    w_conv: bass.AP,
    out: bass.AP,
):
    B, N, D = x.shape
    NB = N // P
    PAIRS = B // S
    K_CHEB = theta.shape[0] // D
    K_CONV = w_conv.shape[2]
    assert D == P and w_att.shape == (D, D) and K_CHEB == 5 and K_CONV == 7 and NB == 8

    x_v = x.rearrange("(q s) (ib p) d -> q s p ib d", s=S, p=P)
    out_v = out.rearrange("(q s) (ib p) d -> q s p ib d", s=S, p=P)
    adj_v = adj.rearrange("(nb p) w -> nb p w", p=P)
    adj_c = adj.rearrange("(nb p) (wb c) -> wb p nb c", p=P, c=P)

    early = nc.dram_tensor("after_relation", (B, N, D), F32, kind="Internal").ap()
    early_v = early.rearrange("(q s) (ib p) d -> q s p ib d", s=S, p=P)
    mid = nc.dram_tensor("after_attention", (B, N, D), F32, kind="Internal").ap()
    mid_v = mid.rearrange("(q s) (ib p) d -> q s p ib d", s=S, p=P)
    dst_row = nc.dram_tensor("dst_row", (S, N), F32, kind="Internal").ap()
    shift_row = nc.dram_tensor("shift_row", (S, 2, N), F32, kind="Internal").ap()

    def wait(eng, sem, value):
        if not isinstance(value, int) or value > 0:
            eng.wait_ge(sem, value)

    ctx = ExitStack()
    with ctx:
        def sb(name, shape, dt=F32, c=ctx):
            return c.enter_context(nc.sbuf_tensor(name, shape, dt))

        def psum(name, shape, c=ctx):
            return c.enter_context(nc.psum_tensor(name, shape, F32))

        def sem(name, c=ctx):
            return c.enter_context(nc.semaphore(name))

        at_hi = sb("at_hi", [P, NB, N], F32R)
        at_lo = sb("at_lo", [P, NB, N], F32R)
        ident = sb("ident", [P, P])
        eps_t = sb("eps_t", [P, S * NB])
        half_t = sb("half_t", [P, S * NB])

        with ExitStack() as c12:
            ones = sb("ones", [P, P], F32, c12)
            mask_n = sb("mask_n", [P, NB, N], BF16, c12)
            mask_t = sb("mask_t", [P, NB, N], BF16, c12)
            w0 = sb("w0", [P, D + 2], F32, c12)
            w1 = sb("w1", [P, D + 2], F32, c12)
            w_r = sb("w_r", [P, 1], F32, c12)
            gb = sb("gb", [P, 1], F32, c12)
            bias0 = sb("bias0", [P, S, D], F32, c12)
            h_ext = sb("h_ext", [P, S, NB, D + 1], F32, c12)

            with ExitStack() as c:
                a_in = sb("a_in", [P, NB, N], F32, c)
                att_w_t = sb("att_w_t", [P, D], F32, c)
                a_sd = sb("a_sd", [P, 2], F32, c)
                tp = psum("tp", [P, 4, 512], c)
                tw = psum("tw", [P, 512], c)
                td = psum("td", [P, 512], c)
                adj_in = [sem(f"adj_in{n}", c) for n in range(NB)]
                w_in = sem("w_in", c)
                g_in = sem("g_in", c)
                att_in = sem("att_in", c)
                zeroed = sem("zeroed", c)
                made = sem("made", c)
                t_ready = sem("t_ready", c)
                hi_done = sem("hi_done", c)
                lo_done = sem("lo_done", c)
                wt_ready = sem("wt_ready", c)
                wt_done = sem("wt_done", c)
                wsd_ready = sem("wsd_ready", c)
                block = c.enter_context(nc.Block())

                @block.sync
                def _(sp):
                    for n in range(NB):
                        sp.dma_start(a_in[:, n, :], adj_v[n]).then_inc(adj_in[n], 16)
                    sp.dma_start(w0[:, 0:D], w_rel).then_inc(w_in, 16)
                    col = g_w.rearrange("(n a) -> n a", a=1)
                    sp.dma_start(w0[:, D:D + 1], col[D:2 * D, :]).then_inc(w_in, 16)
                    sp.dma_start(w0[:, D + 1:D + 2], col[0:D, :]).then_inc(w_in, 16)
                    sp.dma_start(w_r[:], g_w[2 * D:2 * D + 1].partition_broadcast(P)).then_inc(w_in, 16)
                    sp.dma_start(gb[:], g_b.rearrange("(a b) -> a b", a=1)[0].partition_broadcast(P)).then_inc(w_in, 16)
                    for s in range(S):
                        sp.dma_start(bias0[:, s, :], b_rel.partition_broadcast(P)).then_inc(w_in, 16)
                    sp.wait_ge(w_in, 16 * (5 + S))

                @block.gpsimd
                def _(pool):
                    pool.memset(ident[:], 0.0).then_inc(zeroed, 1)
                    pool.wait_ge(zeroed, 1)
                    pool.affine_select(out=ident[:], in_=ident[:], compare_op=ALU.not_equal, fill=1.0,
                                       base=0, pattern=[[-1, P]], channel_multiplier=1).then_inc(made, 1)
                    pool.memset(ones[:], 1.0)
                    pool.memset(eps_t[:], EPS)
                    pool.memset(half_t[:], -0.5)
                    pool.memset(h_ext[:, :, :, D:D + 1], 1.0)

                @block.tensor
                def _(pe):
                    pe.wait_ge(made, 1)
                    pe.wait_ge(att_in, 64)
                    nc.tensor.transpose(tw[:, 0:P], w1[:, 0:D], ident[:]).then_inc(wt_ready, 1)
                    for h in range(2):
                        for jb in range(NB):
                            u = h * NB + jb
                            if u >= 4:
                                pe.wait_ge(lo_done, u - 3)
                            for k in range(4):
                                ib = h * 4 + k
                                if jb == 0:
                                    pe.wait_ge(adj_in[ib], 16)
                                last = nc.tensor.transpose(tp[:, u % 4, k * P:(k + 1) * P],
                                                           a_in[:, ib, jb * P:(jb + 1) * P], ident[:])
                            last.then_inc(t_ready, 1)
                    pe.wait_ge(wt_done, 1)
                    nc.tensor.matmul(td[:, 0:2], att_w_t[:], a_sd[:], start=True, stop=True).then_inc(wsd_ready, 1)

                @block.scalar
                def _(act):
                    act.dma_start(w1[:, 0:D], w_att).then_inc(att_in, 16)
                    act.dma_start(a_sd[:, 0:1], a_src.rearrange("(n a) -> n a", a=1)).then_inc(att_in, 16)
                    act.dma_start(a_sd[:, 1:2], a_dst.rearrange("(n a) -> n a", a=1)).then_inc(att_in, 16)
                    act.dma_start(w1[:, D:D + 1], a_dst.rearrange("(n a) -> n a", a=1)).then_inc(att_in, 16)
                    act.wait_ge(wt_ready, 1)
                    nc.scalar.activation(att_w_t[:], tw[:, 0:P], ACT.Copy).then_inc(wt_done, 1)
                    for u in range(2 * NB):
                        h, jb = u // NB, u % NB
                        act.wait_ge(t_ready, u + 1)
                        nc.scalar.activation(at_hi[:, jb, h * 512:(h + 1) * 512], tp[:, u % 4, :],
                                             ACT.Copy).then_inc(hi_done, 1)
                    act.wait_ge(wsd_ready, 1)
                    nc.scalar.activation(w1[:, D:D + 2], td[:, 0:2], ACT.Copy)

                @block.vector
                def _(dve):
                    for n in range(NB):
                        dve.wait_ge(adj_in[n], 16)
                        nc.vector.tensor_scalar(mask_n[:, n, :], a_in[:, n, :], 0.0, FAR, ALU.is_le, ALU.mult)
                    for u in range(2 * NB):
                        h, jb = u // NB, u % NB
                        half = slice(h * 512, (h + 1) * 512)
                        dve.wait_ge(hi_done, u + 1)
                        nc.vector.tensor_tensor(at_lo[:, jb, half], tp[:, u % 4, :],
                                                at_hi[:, jb, half].bitcast(F32), ALU.subtract).then_inc(lo_done, 1)

            with ExitStack() as c:
                TILES = 8
                x0 = sb("x0", [P, NB, S, D], F32, c)
                x1 = sb("x1", [P, S, NB, D], F32, c)
                x_t = sb("x_t", [P, S, N], F32, c)
                v_f = sb("v_f", [P, NB, S, D], F32, c)
                v_hi = sb("v_hi", [P, NB, S, D], F32R, c)
                v_lo = sb("v_lo", [P, NB, S, D], F32R, c)
                s_ij = sb("s_ij", [P, NB, S, 2], F32, c)
                s_ig = sb("s_ig", [P, NB, S, 1], F32, c)
                sums = sb("sums", [P, 2, S, D], F32, c)
                y_t = sb("y_t", [P, S, D], F32, c)
                stats = sb("stats", [P, S, NB, 6], F32, c)
                mv0 = sb("mv0", [P, S, NB, 2], F32, c)
                mv1 = sb("mv1", [P, NB, 2], F32, c)
                stats1 = sb("stats1", [P, NB, 6], F32, c)
                var_e = sb("var_e", [P, S, NB], F32, c)
                rs0 = sb("rs0", [P, S, NB], F32, c)
                rs1 = sb("rs1", [P, NB], F32, c)
                nm0 = sb("nm0", [P, S, NB], F32, c)
                e_sd = sb("e_sd", [P, S, NB, 2], F32, c)
                e_d2 = sb("e_d2", [P, S, NB], F32, c)
                e_d8 = sb("e_d8", [P, S, NB], F32, c)
                top = sb("top", [P, S, NB], F32, c)
                z_t = sb("z_t", [P, S, NB], F32, c)
                m_t = sb("m_t", [P, S, NB], F32, c)
                shift = sb("shift", [P, S, 2, NB], F32, c)
                dst_bc = sb("dst_bc", [P, N], F32, c)
                shift_bc = sb("shift_bc", [P, 2, N], F32, c)
                junk = sb("junk", [P, N], BF16, c)
                pt = sb("pt", [P, TILES, N], F32, c)
                r_den = sb("r_den", [P, NB], F32, c)

                RING = 5
                ring = psum("ring", [P, RING, 512], c)
                att = psum("att", [P, 3, 512], c)
                GROUPS = [(0, 3), (3, 3), (6, 2)]
                EARLY = 2

                kinds = ["a"] * 4 + ["d"] * 6 + ["d"] + ["d"] * NB + ["a"] * 5 + ["a"] * 5
                U_T, U_V, U_S, U_Y, U_H = 0, 4, 10, 11, 19
                UNITS = len(kinds)
                SLOTS = UNITS + 1
                assert SLOTS % RING == 0
                REL = {k: kinds.count(k) for k in "ad"}
                order = [kinds[:u + 1].count(kinds[u]) for u in range(UNITS)]

                x_in = [sem(f"x_in{s}", c) for s in range(S)]
                unit_ready = sem("unit_ready", c)
                freed = {"a": sem("freed_by_scalar", c), "d": sem("freed_by_vector", c)}
                v_hi_done = sem("v_hi_done", c)
                summed = sem("summed", c)
                mv0_ready = sem("mv0_ready", c)
                rs0_ready = sem("rs0_ready", c)
                shift0_ready = sem("shift0_ready", c)
                x1_ready = [sem(f"x1_ready{s}", c) for s in range(S)]
                moved = [sem(f"moved{s}", c) for s in range(S)]
                x1_in = [sem(f"x1_in{s}", c) for s in range(S)]
                dst_out = sem("dst_out", c)
                dst_in = sem("dst_in", c)
                shift_ready = sem("shift_ready", c)
                shift_out = sem("shift_out", c)
                shift_in = sem("shift_in", c)
                tile_free = sem("tile_free", c)
                leaky_done = sem("leaky_done", c)
                masked = sem("masked", c)
                exp_done = sem("exp_done", c)
                att_free = sem("att_free", c)
                mv1_ready = sem("mv1_ready", c)
                rs1_ready = sem("rs1_ready", c)
                x2_ready = [sem(f"x2_ready{s}", c) for s in range(S)]
                step = sem("step", c)
                pool_step = sem("pool_step", c)
                block = c.enter_context(nc.Block())

                def v_view(bank, n):
                    return ring[:, bank, 0:n * (D + 2)].rearrange("p (k c) -> p k c", c=D + 2)

                @block.sync
                def _(sp):
                    def load_x(p, s):
                        sp.dma_start(x0[:, :, s, :], x_v[p, s]).then_inc(x_in[s], 16)

                    def spread_dst(p, s):
                        sp.wait_ge(freed["a"], p * REL["a"] + order[U_H + 5 * s + 4])
                        sp.dma_start(dst_row[s].rearrange("(ib p) -> p ib", p=P), e_sd[:, s, :, 1],
                                     allow_slow_non_contiguous=True).then_inc(dst_out, 16)
                        wait(sp, shift_ready, p * S + s)
                        sp.wait_ge(dst_out, p * (16 * S) + (16 * s + 16))
                        sp.dma_start(dst_bc[:], dst_row[s].partition_broadcast(P)).then_inc(dst_in, 16)

                    def spread_shift(p, s):
                        sp.wait_ge(shift_ready, p * S + (s + 1))
                        for k in range(2):
                            sp.dma_start(shift_row[s, k].rearrange("(ib p) -> p ib", p=P), shift[:, s, k, :],
                                         allow_slow_non_contiguous=True).then_inc(shift_out, 16)
                        sp.wait_ge(shift_out, p * (32 * S) + (32 * s + 32))
                        for k in range(2):
                            sp.dma_start(shift_bc[:, k, :], shift_row[s, k].partition_broadcast(P)).then_inc(shift_in, 16)

                    def store(p, s):
                        sp.wait_ge(x2_ready[s], p + 1)
                        sp.dma_start(mid_v[p, s], x1[:, s, :, :]).then_inc(moved[s], 16)

                    def save(p, s):
                        sp.wait_ge(x1_ready[s], p + 1)
                        sp.dma_start(early_v[p, s], x0[:, :, s, :]).then_inc(moved[s], 16)

                    def residual(p, s):
                        sp.wait_ge(moved[s], p * 32 + 16)
                        sp.dma_start(x1[:, s, :, :], early_v[p, s]).then_inc(x1_in[s], 16)

                    def reload(p, s):
                        sp.wait_ge(freed["a"], (p - 1) * REL["a"] + order[U_H + 5 * s + 1])
                        load_x(p, s)

                    def steady(p, more):
                        spread_dst(p, 1)
                        spread_shift(p, 1)
                        for s in range(S):
                            save(p + 1, s)
                        store(p, 0)
                        residual(p + 1, 0)
                        spread_dst(p + 1, 0)
                        if more:
                            for s in range(S):
                                reload(p + 2, s)
                        spread_shift(p + 1, 0)
                        store(p, 1)
                        residual(p + 1, 1)

                    for s in range(S):
                        load_x(0, s)
                    for s in range(S):
                        save(0, s)
                        residual(0, s)
                    spread_dst(0, 0)
                    for s in range(S):
                        reload(1, s)
                    spread_shift(0, 0)
                    with sp.Fori(0, PAIRS - 2) as p:
                        steady(p, True)
                    steady(PAIRS - 2, False)
                    spread_dst(PAIRS - 1, 1)
                    spread_shift(PAIRS - 1, 1)
                    for s in range(S):
                        store(PAIRS - 1, s)
                    for s in range(S):
                        sp.wait_ge(moved[s], 32 * PAIRS)

                @block.tensor
                def _(pe):
                    def bank(p, u):
                        before = u - RING
                        if before < 0:
                            before = before + SLOTS
                            p = p - 1
                        if before == UNITS:
                            before -= RING
                        if not (isinstance(p, int) and p < 0):
                            wait(pe, freed[kinds[before]], p * REL[kinds[before]] + order[before])
                        return u % RING

                    def transposes(p, u, s):
                        for half in range(2):
                            b = bank(p, u + half)
                            for k in range(4):
                                last = nc.tensor.transpose(ring[:, b, k * P:(k + 1) * P],
                                                           x0[:, half * 4 + k, s, :], ident[:])
                            last.then_inc(unit_ready, 1)

                    def project(p, u, u_t, s, w):
                        wait(pe, freed["a"], p * REL["a"] + order[u_t + 1])
                        for g, (b0, n) in enumerate(GROUPS):
                            b = bank(p, u + g)
                            for k in range(n):
                                last = nc.tensor.matmul(v_view(b, n)[:, k, :], x_t[:, s, (b0 + k) * P:(b0 + k + 1) * P],
                                                        w[:], start=True, stop=True)
                            last.then_inc(unit_ready, 1)

                    def relation(p):
                        for s in range(S):
                            pe.wait_ge(x_in[s], p * 16 + 16)
                            transposes(p, U_T + 2 * s, s)
                        for s in range(S):
                            project(p, U_V + 3 * s, U_T + 2 * s, s, w0)
                        b = bank(p, U_S)
                        wait(pe, freed["d"], p * REL["d"] + order[U_S - 1])
                        for jb in range(NB):
                            nc.tensor.matmul(ring[:, b, 0:S * D], ones[:], v_f[:, jb, :, :].rearrange("p s d -> p (s d)"),
                                             start=(jb == 0), stop=(jb == NB - 1))
                        for s in range(S):
                            for jb in range(NB):
                                last = nc.tensor.matmul(ring[:, b, (S + s) * D:(S + s + 1) * D],
                                                        s_ij[:, jb, s, 1:2].to_broadcast([P, P]), v_f[:, jb, s, :],
                                                        start=(jb == 0), stop=(jb == NB - 1))
                        last.then_inc(unit_ready, 1)
                        for ib in range(NB):
                            b = bank(p, U_Y + ib)
                            for jb in range(NB):
                                for n, (a, v) in enumerate(((at_hi, v_hi), (at_hi, v_lo), (at_lo, v_hi))):
                                    last = nc.tensor.matmul(ring[:, b, 0:S * D], a[:, jb, ib * P:(ib + 1) * P],
                                                            v[:, jb, :, :].rearrange("p s d -> p (s d)"),
                                                            start=(jb == 0 and n == 0), stop=(jb == NB - 1 and n == 2))
                            last.then_inc(unit_ready, 1)

                    def heads(p, s):
                        pe.wait_ge(x1_ready[s], p + 1)
                        transposes(p, U_H + 5 * s, s)
                        project(p, U_H + 5 * s + 2, U_H + 5 * s, s, w1)

                    def attend(p, s):
                        pe.wait_ge(att_free, p * S + (s + 1))
                        for jb in range(NB):
                            pe.wait_ge(exp_done, p * (S * NB) + (s * NB + jb + 1))
                            for g, (b0, n) in enumerate(GROUPS):
                                for k in range(n):
                                    last = nc.tensor.matmul(
                                        att[:, g, k * (D + 1):(k + 1) * (D + 1)],
                                        pt[:, jb % TILES, (b0 + k) * P:(b0 + k + 1) * P], h_ext[:, s, jb, :],
                                        start=(jb == 0 and k == 0), stop=(jb == NB - 1), skip_group_check=True)
                            last.then_inc(tile_free, 1)

                    pe.sem_inc(att_free, 1)
                    pe.sem_inc(tile_free, TILES)
                    relation(0)
                    for s in range(S):
                        heads(0, s)
                    with pe.Fori(0, PAIRS - 1) as p:
                        relation(p + 1)
                        for s in range(S):
                            attend(p, s)
                            heads(p + 1, s)
                    for s in range(S):
                        attend(PAIRS - 1, s)

                @block.scalar
                def _(act):
                    def copy_t(p, u, s):
                        for half in range(2):
                            act.wait_ge(unit_ready, p * UNITS + (u + half + 1))
                            nc.scalar.activation(x_t[:, s, half * 512:(half + 1) * 512], ring[:, (u + half) % RING, :],
                                                 ACT.Copy).then_inc(freed["a"], 1)

                    def relation(p):
                        for s in range(S):
                            copy_t(p, U_T + 2 * s, s)
                        for s in range(S):
                            for g, (b0, n) in enumerate(GROUPS):
                                u = U_V + 3 * s + g
                                act.wait_ge(unit_ready, p * UNITS + (u + 1))
                                src = v_view(u % RING, n)[:, :, 0:D]
                                nc.scalar.activation(v_f[:, b0:b0 + n, s, :], src, ACT.Copy)
                                nc.scalar.activation(v_hi[:, b0:b0 + n, s, :], src, ACT.Copy,
                                                     scale=w_r[:, 0:1]).then_inc(v_hi_done, 1)

                    def heads(p, s):
                        u = U_H + 5 * s
                        copy_t(p, u, s)
                        for g, (b0, n) in enumerate(GROUPS):
                            act.wait_ge(unit_ready, p * UNITS + (u + 2 + g + 1))
                            src = v_view((u + 2 + g) % RING, n)
                            nc.scalar.activation(h_ext[:, s, b0:b0 + n, 0:D], src[:, :, 0:D], ACT.Copy)
                            nc.scalar.activation(e_sd[:, s, b0:b0 + n, :], src[:, :, D:D + 2],
                                                 ACT.Copy).then_inc(freed["a"], 1)

                    def norm(p):
                        for s in range(S):
                            act.wait_ge(shift0_ready, p * S + (s + 1))
                            for ib in range(NB):
                                last = nc.scalar.activation(x0[:, ib, s, :], x0[:, ib, s, :], ACT.Identity,
                                                            bias=nm0[:, s, ib:ib + 1], scale=rs0[:, s, ib:ib + 1])
                            last.then_inc(x1_ready[s], 1)

                    def expo(p, s, b0, b1):
                        for jb in range(b0, b1):
                            act.wait_ge(masked, p * (S * NB) + (s * NB + jb + 1))
                            nc.scalar.activation(pt[:, jb % TILES, :], pt[:, jb % TILES, :], ACT.Exp,
                                                 bias=e_d2[:, s, jb:jb + 1]).then_inc(exp_done, 1)

                    relation(0)
                    norm(0)
                    for s in range(S):
                        heads(0, s)
                    with act.Fori(0, PAIRS - 1) as p:
                        relation(p + 1)
                        expo(p, 0, 0, NB)
                        norm(p + 1)
                        expo(p, 1, 0, EARLY)
                        heads(p + 1, 0)
                        expo(p, 1, EARLY, NB)
                        heads(p + 1, 1)
                    for s in range(S):
                        expo(PAIRS - 1, s, 0, NB)

                @block.vector
                def _(dve):
                    count = [0]

                    def link(ins):
                        count[0] += 1
                        ins.then_inc(step, 1)
                        dve.wait_ge(step, count[0])

                    def restart():
                        dve.sem_clear(step)
                        count[0] = 0

                    def project(p):
                        for s in range(S):
                            for g, (b0, n) in enumerate(GROUPS):
                                u = U_V + 3 * s + g
                                src = v_view(u % RING, n)
                                dve.wait_ge(v_hi_done, p * (2 * 3) + (s * 3 + g + 1))
                                nc.vector.scalar_tensor_tensor(
                                    out=v_lo[:, b0:b0 + n, s, :], in0=src[:, :, 0:D], scalar=w_r[:, 0:1],
                                    in1=v_hi[:, b0:b0 + n, s, :].bitcast(F32), op0=ALU.mult, op1=ALU.subtract)
                                nc.vector.tensor_copy(s_ij[:, b0:b0 + n, s, :], src[:, :, D:D + 2]).then_inc(freed["d"], 1)
                        dve.wait_ge(freed["d"], p * REL["d"] + order[U_S - 1])
                        nc.vector.tensor_scalar(s_ig[:], s_ij[:, :, :, 0:1], gb[:, 0:1], None, ALU.add)
                        dve.wait_ge(unit_ready, p * UNITS + (U_S + 1))
                        src = ring[:, U_S % RING, :].rearrange("p (k s d) -> p k s d", k=2, s=S)
                        nc.vector.tensor_copy(sums[:, 0, :, :], src[:, 0, :, :])
                        nc.vector.tensor_tensor(sums[:, 1, :, :], src[:, 1, :, :], bias0[:], ALU.add).then_inc(freed["d"], 1)

                    def rows(p, b0, b1):
                        for ib in range(b0, b1):
                            u = U_Y + ib
                            dve.wait_ge(unit_ready, p * UNITS + (u + 1))
                            if ib == 0:
                                dve.wait_ge(summed, p * S + S)
                            for s in range(S):
                                last = nc.vector.scalar_tensor_tensor(
                                    out=y_t[:, s, :], in0=sums[:, 0, s, :], scalar=s_ig[:, ib, s, :],
                                    in1=ring[:, u % RING, s * D:(s + 1) * D], op0=ALU.mult, op1=ALU.add)
                            last.then_inc(freed["d"], 1)
                            dve.wait_ge(freed["d"], p * REL["d"] + order[u])
                            link(nc.vector.tensor_tensor(x0[:, ib, :, :], y_t[:], x0[:, ib, :, :], ALU.add))
                            for s in range(S):
                                last = nc.vector.bn_stats(stats[:, s, ib, :], x0[:, ib, s, :])
                            link(last)

                    def norm0(p):
                        for s in range(S):
                            for ib in range(NB):
                                last = nc.vector.bn_aggr(mv0[:, s, ib, :], stats[:, s, ib, :])
                            last.then_inc(mv0_ready, 1)
                        for s in range(S):
                            dve.wait_ge(rs0_ready, p * S + (s + 1))
                            nc.vector.scalar_tensor_tensor(out=nm0[:, s, :], in0=mv0[:, s, :, 0], scalar=-1.0,
                                                           in1=rs0[:, s, :], op0=ALU.mult,
                                                           op1=ALU.mult).then_inc(shift0_ready, 1)

                    def maximum(p, s):
                        dve.wait_ge(dst_in, p * (16 * S) + (16 * s + 16))
                        nc.vector.tensor_scalar(e_d2[:, s, :], e_sd[:, s, :, 1], SLOPE, None, ALU.mult)
                        nc.vector.tensor_scalar(e_d8[:, s, :], e_sd[:, s, :, 1], 1.0 - SLOPE, None, ALU.mult)
                        for ib in range(NB):
                            link(nc.vector.tensor_tensor_reduce(junk[:], mask_n[:, ib, :], dst_bc[:], 1.0,
                                                                3 * FAR, ALU.add, ALU.max, top[:, s, ib:ib + 1]))
                        src = e_sd[:, s, :, 0]
                        link(nc.vector.tensor_tensor(z_t[:, s, :], src, top[:, s, :], ALU.add))
                        link(nc.vector.scalar_tensor_tensor(out=m_t[:, s, :], in0=z_t[:, s, :], scalar=SLOPE,
                                                            in1=z_t[:, s, :], op0=ALU.mult, op1=ALU.max))
                        nc.vector.tensor_tensor(shift[:, s, 0, :], src, m_t[:, s, :], ALU.subtract)
                        nc.vector.scalar_tensor_tensor(out=shift[:, s, 1, :], in0=src, scalar=SLOPE, in1=m_t[:, s, :],
                                                       op0=ALU.mult, op1=ALU.subtract).then_inc(shift_ready, 1)

                    def scores(p, s, b0, b1):
                        if b0 == 0:
                            dve.wait_ge(shift_in, p * (32 * S) + (32 * s + 32))
                        for jb in range(b0, b1 + 1):
                            tile, before = pt[:, jb % TILES, :], pt[:, (jb - 1) % TILES, :]
                            if jb < b1:
                                dve.wait_ge(tile_free, p * (S * NB) + (s * NB + jb + 1))
                                nc.vector.scalar_tensor_tensor(out=tile, in0=shift_bc[:, 0, :], scalar=e_d8[:, s, jb:jb + 1],
                                                               in1=shift_bc[:, 1, :], op0=ALU.add,
                                                               op1=ALU.max).then_inc(leaky_done, 1)
                            if jb > b0:
                                dve.wait_ge(leaky_done, p * (S * NB) + (s * NB + jb))
                                nc.vector.tensor_tensor(before, before, mask_t[:, jb - 1, :], ALU.add).then_inc(masked, 1)

                    def finish(p, s):
                        dve.wait_ge(tile_free, p * (S * NB) + (s * NB + NB + TILES))
                        dve.wait_ge(x1_in[s], p * 16 + 16)
                        for g, (b0, n) in enumerate(GROUPS):
                            src = att[:, g, 0:n * (D + 1)].rearrange("p (k c) -> p k c", c=D + 1)
                            last = nc.vector.reciprocal(r_den[:, b0:b0 + n], src[:, :, D])
                        link(last)
                        for g, (b0, n) in enumerate(GROUPS):
                            for k in range(n):
                                last = nc.vector.scalar_tensor_tensor(
                                    out=x1[:, s, b0 + k, :], in0=att[:, g, k * (D + 1):k * (D + 1) + D],
                                    scalar=r_den[:, b0 + k:b0 + k + 1], in1=x1[:, s, b0 + k, :], op0=ALU.mult, op1=ALU.add)
                        last.then_inc(att_free, 1)
                        dve.wait_ge(att_free, p * S + (s + 2))
                        for ib in range(NB):
                            last = nc.vector.bn_stats(stats1[:, ib, :], x1[:, s, ib, :])
                        link(last)
                        for ib in range(NB):
                            last = nc.vector.bn_aggr(mv1[:, ib, :], stats1[:, ib, :])
                        last.then_inc(mv1_ready, 1)
                        dve.wait_ge(rs1_ready, p * S + (s + 1))
                        for ib in range(NB):
                            last = nc.vector.tensor_scalar(x1[:, s, ib, :], x1[:, s, ib, :], mv1[:, ib, 0:1],
                                                           rs1[:, ib:ib + 1], ALU.subtract, ALU.mult)
                        last.then_inc(x2_ready[s], 1)

                    project(0)
                    rows(0, 0, NB)
                    norm0(0)
                    for jb in range(NB):
                        nc.vector.tensor_scalar(mask_t[:, jb, :], at_hi[:, jb, :].bitcast(F32), 0.0, FAR,
                                                ALU.is_le, ALU.mult)
                    maximum(0, 0)
                    restart()
                    with dve.Fori(0, PAIRS - 1) as p:
                        project(p + 1)
                        scores(p, 0, 0, NB)
                        rows(p + 1, 0, NB // 2)
                        maximum(p, 1)
                        rows(p + 1, NB // 2, NB)
                        norm0(p + 1)
                        scores(p, 1, 0, EARLY)
                        finish(p, 0)
                        scores(p, 1, EARLY, NB)
                        maximum(p + 1, 0)
                        finish(p, 1)
                        restart()
                    scores(PAIRS - 1, 0, 0, NB)
                    maximum(PAIRS - 1, 1)
                    scores(PAIRS - 1, 1, 0, EARLY)
                    finish(PAIRS - 1, 0)
                    scores(PAIRS - 1, 1, EARLY, NB)
                    finish(PAIRS - 1, 1)

                @block.gpsimd
                def _(pool):
                    def add_sums(p):
                        pool.wait_ge(freed["d"], p * REL["d"] + order[U_S])
                        for s in range(S):
                            row = sums[:, 1, s, :].unsqueeze(1).broadcast_to([P, NB, D])
                            pool.tensor_tensor(x0[:, :, s, :], x0[:, :, s, :], row, ALU.add).then_inc(summed, 1)

                    def root(mv, var_at, rs, ready, value, done):
                        pool.wait_ge(ready, value)
                        pool.tensor_tensor(var_at, mv, eps_t[:, 0:NB], ALU.add).then_inc(pool_step, 1)
                        pool.wait_ge(pool_step, 1)
                        pool.sem_clear(pool_step)
                        pool.tensor_tensor(rs, var_at, half_t[:, 0:NB], ALU.pow).then_inc(done, 1)

                    def relation(p):
                        add_sums(p)
                        for s in range(S):
                            root(mv0[:, s, :, 1], var_e[:, s, :], rs0[:, s, :], mv0_ready, p * S + (s + 1), rs0_ready)

                    def finish(p, s):
                        root(mv1[:, :, 1], var_e[:, s, :], rs1[:], mv1_ready, p * S + (s + 1), rs1_ready)

                    relation(0)
                    with pool.Fori(0, PAIRS - 1) as p:
                        relation(p + 1)
                        for s in range(S):
                            finish(p, s)
                    for s in range(S):
                        finish(PAIRS - 1, s)

        with ExitStack() as c:
            a_hi = sb("a_hi", [P, NB, N], F32R, c)
            a_lo = sb("a_lo", [P, NB, N], F32R, c)
            STAGE = 3
            a_in = sb("a_part", [P, STAGE, NB, P], F32, c)
            xin = sb("xin", [P, NB, S, D], F32, c)
            xb = sb("xb", [P, NB, S, D], F32, c)
            x_t = sb("x_t3", [P, NB, S, D], F32, c)
            z_hi = sb("z_hi", [P, 2, NB, S, D], F32R, c)
            z_lo = sb("z_lo", [P, 2, NB, S, D], F32R, c)
            y_t = sb("y_t3", [P, S, D], F32, c)
            w_all = sb("w_all", [P, K_CONV * D], F32, c)
            w2 = sb("w2", [P, 3, D], F32, c)
            w3 = sb("w3", [P, 4, D], F32, c)
            bias2 = sb("bias2", [P, S, D], F32, c)
            stats = sb("stats3", [P, 2, S, 6], F32, c)
            mv = sb("mv3", [P, 2, S, 2], F32, c)
            var_e = sb("var_e3", [P, 2, S], F32, c)
            rs = sb("rs3", [P, 2, S], F32, c)
            RING = 8
            ring = psum("ring3", [P, RING, 512], c)

            HOPS = (2, 3)
            kinds, base = [], []
            for hops in HOPS:
                base.append(len(kinds))
                kinds += ["a"] * (NB // 2) + ["d"] * (NB * (1 + hops))
            UNITS = len(kinds)
            assert UNITS % RING == 0
            REL = {k: kinds.count(k) for k in "ad"}
            order = [kinds[:u + 1].count(kinds[u]) for u in range(UNITS)]
            SPLITS = NB * sum(HOPS)

            adj_in = [sem(f"adj_part{n}", c) for n in range(STAGE)]
            a_hi_done = sem("a_hi_done", c)
            a_lo_done = sem("a_lo_done", c)
            theta_in = sem("theta_in", c)
            conv_in = sem("conv_in", c)
            w2_ready = sem("w2_ready", c)
            w3_ready = sem("w3_ready", c)
            bias_in = sem("bias_in", c)
            x_in = sem("xin_in", c)
            copied = sem("copied", c)
            unit_ready = sem("unit_ready3", c)
            freed = {"a": sem("freed_by_scalar3", c), "d": sem("freed_by_vector3", c)}
            split_hi = sem("split_hi", c)
            mv_ready = sem("mv_ready3", c)
            rs_ready = sem("rs_ready3", c)
            normed = sem("normed", c)
            stored = sem("stored3", c)
            step = sem("step3", c)
            pool_step = sem("pool_step3", c)
            block = c.enter_context(nc.Block())
            BLOCKS = len(HOPS) * NB

            @block.sync
            def _(sp):
                def load_x(q):
                    for s in range(S):
                        sp.dma_start(xin[:, :, s, :], mid_v[q, s]).then_inc(x_in, 16)

                def store(q):
                    sp.wait_ge(normed, q * BLOCKS + BLOCKS)
                    for s in range(S):
                        sp.dma_start(out_v[q, s], xb[:, :, s, :]).then_inc(stored, 16)

                load_x(0)
                for s in range(S):
                    sp.dma_start(bias2[:, s, :], b_cheb.partition_broadcast(P)).then_inc(bias_in, 16)
                for n in range(NB):
                    if n >= STAGE:
                        sp.wait_ge(a_lo_done, n - STAGE + 1)
                    sp.dma_start(a_in[:, n % STAGE, :, :], adj_c[n]).then_inc(adj_in[n % STAGE], 16)
                with sp.Fori(0, PAIRS - 1) as q:
                    sp.wait_ge(copied, q + 1)
                    load_x(q + 1)
                    store(q)
                store(PAIRS - 1)
                sp.wait_ge(stored, 16 * S * PAIRS)

            @block.tensor
            def _(pe):
                def bank(q, u):
                    before = u - RING
                    if before < 0:
                        before, q = before + UNITS, q - 1
                    if not (isinstance(q, int) and q < 0):
                        wait(pe, freed[kinds[before]], q * REL[kinds[before]] + order[before])
                    return u % RING

                def times_w(q, b, ib, w, start):
                    for s in range(S):
                        last = nc.tensor.matmul(ring[:, b, s * D:(s + 1) * D], x_t[:, ib, s, :], w,
                                                start=start, stop=(start or s == S - 1))
                    return last

                def layer(q, n, src, a_h, a_l, w):
                    u = base[n]

                    def transposes(t):
                        if n == 0 and t == 0:
                            pe.wait_ge(x_in, q * (16 * S) + 16 * S)
                        if n == 1:
                            pe.wait_ge(normed, q * BLOCKS + (2 * t + 2))
                        b = bank(q, u + t)
                        for k in range(2):
                            for s in range(S):
                                last = nc.tensor.transpose(ring[:, b, (k * S + s) * P:(k * S + s + 1) * P],
                                                           src[:, 2 * t + k, s, :], ident[:])
                        last.then_inc(unit_ready, 1)

                    for t in range(NB // 2):
                        transposes(t)
                    u += NB // 2
                    if isinstance(q, int) and q == 0:
                        pe.wait_ge((w2_ready, w3_ready)[n], 1)
                    for ib in range(NB):
                        if ib % 2 == 0:
                            wait(pe, freed["a"], q * REL["a"] + order[base[n] + ib // 2])
                        b = bank(q, u + ib)
                        times_w(q, b, ib, w[:, 0, :], True).then_inc(unit_ready, 1)
                    for hop in range(HOPS[n]):
                        u += NB
                        for ib in range(NB):
                            if isinstance(q, int) and q == 0 and n == 0 and hop == 0:
                                pe.wait_ge(a_lo_done, ib + 1)
                            b = bank(q, u + ib)
                            for jb in range(NB):
                                if ib == 0:
                                    wait(pe, freed["d"], q * REL["d"] + order[u - NB + jb])
                                for k, (a, z) in enumerate(((a_h, z_hi), (a_h, z_lo), (a_l, z_hi))):
                                    nc.tensor.matmul(ring[:, b, 0:S * D], a[:, jb, ib * P:(ib + 1) * P],
                                                     z[:, hop % 2, jb, :, :].rearrange("p s d -> p (s d)"),
                                                     start=(jb == 0 and k == 0), stop=False)
                            times_w(q, b, ib, w[:, hop + 1, :], False).then_inc(unit_ready, 1)

                def pair(q):
                    layer(q, 0, xin, a_hi, a_lo, w2)
                    layer(q, 1, xb, at_hi, at_lo, w3)

                pair(0)
                with pe.Fori(1, PAIRS) as q:
                    pair(q)

            @block.scalar
            def _(act):
                def layer(q, n):
                    u = base[n]
                    for t in range(NB // 2):
                        act.wait_ge(unit_ready, q * UNITS + (u + t + 1))
                        nc.scalar.activation(x_t[:, 2 * t:2 * t + 2, :, :].rearrange("p k s d -> p (k s d)"),
                                             ring[:, (u + t) % RING, :], ACT.Copy).then_inc(freed["a"], 1)
                    u += NB // 2
                    for k in range(HOPS[n]):
                        for ib in range(NB):
                            act.wait_ge(unit_ready, q * UNITS + (u + ib + 1))
                            nc.scalar.activation(z_hi[:, k % 2, ib, :, :].rearrange("p s d -> p (s d)"),
                                                 ring[:, (u + ib) % RING, 0:S * D], ACT.Copy).then_inc(split_hi, 1)
                        u += NB
                        if isinstance(q, int) and q == 0 and n == 0 and k == 0:
                            for i in range(NB):
                                act.wait_ge(adj_in[i % STAGE], 16 * (i // STAGE + 1))
                                nc.scalar.activation(a_hi[:, :, i * P:(i + 1) * P], a_in[:, i % STAGE, :, :],
                                                     ACT.Copy).then_inc(a_hi_done, 1)
                        if n == 0 and k == 0:
                            wait(act, stored, q * (16 * S))
                            nc.scalar.activation(xb[:], xin[:], ACT.Copy).then_inc(copied, 1)

                def pair(q):
                    layer(q, 0)
                    layer(q, 1)

                act.dma_start(w_all[:, 0:K_CHEB * D].rearrange("p (k o) -> p k o", o=D),
                              theta.rearrange("(k f) o -> f k o", f=D)).then_inc(theta_in, 16)
                act.wait_ge(w2_ready, 1)
                act.dma_start(w_all[:], w_conv.rearrange("i o k -> i (o k)")).then_inc(conv_in, 16)
                pair(0)
                with act.Fori(1, PAIRS) as q:
                    pair(q)

            @block.vector
            def _(dve):
                count = [0]

                def link(ins):
                    count[0] += 1
                    ins.then_inc(step, 1)
                    dve.wait_ge(step, count[0])

                def weights():
                    dve.wait_ge(theta_in, 16)
                    th = w_all[:, 0:K_CHEB * D].rearrange("p (k o) -> p k o", o=D)
                    nc.vector.tensor_tensor(w2[:, 1, :], th[:, 1, :], th[:, 3, :], ALU.add)
                    link(nc.vector.tensor_tensor(w2[:, 0, :], th[:, 2, :], th[:, 4, :], ALU.add))
                    link(nc.vector.tensor_tensor(w2[:, 2, :], th[:, 0, :], w2[:, 0, :], ALU.subtract))
                    nc.vector.tensor_scalar(w2[:, 0, :], w2[:, 0, :], 2.0, None, ALU.mult).then_inc(w2_ready, 1)
                    dve.wait_ge(conv_in, 16)
                    cv = w_all[:].rearrange("p (o k) -> p k o", k=K_CONV)
                    nc.vector.tensor_copy(w3[:, 3, :], cv[:, 0, :])
                    for k in range(3):
                        last = nc.vector.tensor_tensor(w3[:, 2 - k, :], cv[:, 1 + k, :], cv[:, 4 + k, :], ALU.add)
                    last.then_inc(w3_ready, 1)

                def stats_of(ib):
                    for s in range(S):
                        last = nc.vector.bn_stats(stats[:, ib % 2, s, :], xb[:, ib, s, :])
                    link(last)
                    for s in range(S):
                        last = nc.vector.bn_aggr(mv[:, ib % 2, s, :], stats[:, ib % 2, s, :])
                    last.then_inc(mv_ready, 1)

                def norm(q, n, ib):
                    dve.wait_ge(rs_ready, q * BLOCKS + (n * NB + ib + 1))
                    for s in range(S):
                        last = nc.vector.tensor_scalar(xb[:, ib, s, :], xb[:, ib, s, :], mv[:, ib % 2, s, 0:1],
                                                       rs[:, ib % 2, s:s + 1], ALU.subtract, ALU.mult)
                    last.then_inc(normed, 1)

                def layer(q, n):
                    u = base[n] + NB // 2
                    done = NB * sum(HOPS[:n])
                    for k in range(HOPS[n]):
                        for ib in range(NB):
                            dve.wait_ge(split_hi, q * SPLITS + (done + k * NB + ib + 1))
                            nc.vector.tensor_tensor(z_lo[:, k % 2, ib, :, :].rearrange("p s d -> p (s d)"),
                                                    ring[:, (u + ib) % RING, 0:S * D],
                                                    z_hi[:, k % 2, ib, :, :].rearrange("p s d -> p (s d)").bitcast(F32),
                                                    ALU.subtract).then_inc(freed["d"], 1)
                        u += NB
                        if isinstance(q, int) and q == 0 and n == 0 and k == 0:
                            for i in range(NB):
                                dve.wait_ge(a_hi_done, i + 1)
                                nc.vector.tensor_tensor(a_lo[:, :, i * P:(i + 1) * P], a_in[:, i % STAGE, :, :],
                                                        a_hi[:, :, i * P:(i + 1) * P].bitcast(F32),
                                                        ALU.subtract).then_inc(a_lo_done, 1)
                    for ib in range(NB):
                        if n == 0 and ib == 0:
                            dve.wait_ge(copied, q + 1)
                        dve.wait_ge(unit_ready, q * UNITS + (u + ib + 1))
                        got = ring[:, (u + ib) % RING, 0:S * D].rearrange("p (s d) -> p s d", s=S)
                        if n == 0:
                            nc.vector.tensor_tensor(y_t[:], got, bias2[:], ALU.add).then_inc(freed["d"], 1)
                            dve.wait_ge(freed["d"], q * REL["d"] + order[u + ib])
                            link(nc.vector.scalar_tensor_tensor(out=xb[:, ib, :, :].rearrange("p s d -> p (s d)"),
                                                                in0=y_t[:].rearrange("p s d -> p (s d)"), scalar=0.0,
                                                                in1=xb[:, ib, :, :].rearrange("p s d -> p (s d)"),
                                                                op0=ALU.max, op1=ALU.add))
                        else:
                            nc.vector.tensor_tensor(xb[:, ib, :, :], got, xb[:, ib, :, :], ALU.add).then_inc(freed["d"], 1)
                            dve.wait_ge(freed["d"], q * REL["d"] + order[u + ib])
                        stats_of(ib)
                        if ib > 0:
                            norm(q, n, ib - 1)
                    norm(q, n, NB - 1)

                def pair(q):
                    layer(q, 0)
                    layer(q, 1)
                    dve.sem_clear(step)
                    count[0] = 0

                weights()
                dve.wait_ge(bias_in, 16 * S)
                pair(0)
                with dve.Fori(1, PAIRS) as q:
                    pair(q)

            @block.gpsimd
            def _(pool):
                def roots(q):
                    for n in range(BLOCKS):
                        k = n % 2
                        pool.wait_ge(mv_ready, q * BLOCKS + (n + 1))
                        pool.tensor_tensor(var_e[:, k, :], mv[:, k, :, 1], eps_t[:, 0:S], ALU.add).then_inc(pool_step, 1)
                        pool.wait_ge(pool_step, 1)
                        pool.sem_clear(pool_step)
                        pool.tensor_tensor(rs[:, k, :], var_e[:, k, :], half_t[:, 0:S], ALU.pow).then_inc(rs_ready, 1)

                with pool.Fori(0, PAIRS) as q:
                    roots(q)


_INS = ['x', 'adj', 'L0_gnn_g_w', 'L0_gnn_g_b', 'L0_gnn_weight', 'L0_gnn_bias', 'L1_gnn_w', 'L1_gnn_a_src',
        'L1_gnn_a_dst', 'L2_gnn_Theta1', 'L2_gnn_bias', 'L3_gnn_weight_1']
_OUTS = [((8, 1024, 128), 'float32')]


def kernel(**inputs):
    import numpy as _np
    import concourse.bacc as _bacc
    from concourse import mybir as _mybir
    from concourse.bass_utils import run_bass_kernel_spmd as _run

    nc = _bacc.Bacc("TRN2", target_bir_lowering=False, num_devices=1)
    arrays, args = {}, []
    for name in _INS:
        a = _np.ascontiguousarray(inputs[name]).reshape(_np.shape(inputs[name]) or (1,))
        arrays[f"in_{name}_dram"] = a
        args.append(nc.dram_tensor(f"in_{name}_dram", a.shape, _mybir.dt.from_np(a.dtype), kind="ExternalInput").ap())
    for i, (shape, dtype) in enumerate(_OUTS):
        dt = _mybir.dt.from_np(_np.dtype(dtype))
        args.append(nc.dram_tensor(f"out_{i}_dram", shape, dt, kind="ExternalOutput").ap())
    gnn_kernel(nc, *args)
    r = _run(nc, [arrays], core_ids=[0])
    got = tuple(r.results[0][f"out_{i}_dram"] for i in range(len(_OUTS)))
    return got[0]
```

```python
from contextlib import ExitStack

import concourse.bass as bass
from concourse import mybir

ALU = mybir.AluOpType
ACT = mybir.ActivationFunctionType
F32 = mybir.dt.float32
F32R = mybir.dt.float32r
BF16 = mybir.dt.bfloat16

P = 128
S = 2
EPS = 1e-5
SLOPE = 0.2
FAR = -1e30


def gnn_kernel(
    nc: bass.Bass,
    x: bass.AP,
    adj: bass.AP,
    g_w: bass.AP,
    g_b: bass.AP,
    w_rel: bass.AP,
    b_rel: bass.AP,
    w_att: bass.AP,
    a_src: bass.AP,
    a_dst: bass.AP,
    theta: bass.AP,
    b_cheb: bass.AP,
    w_conv: bass.AP,
    out: bass.AP,
):
    B, N, D = x.shape
    NB = N // P
    PAIRS = B // S
    K_CHEB = theta.shape[0] // D
    K_CONV = w_conv.shape[2]
    assert D == P and w_att.shape == (D, D) and K_CHEB == 5 and K_CONV == 7 and NB == 8

    x_v = x.rearrange("(q s) (ib p) d -> q s p ib d", s=S, p=P)
    out_v = out.rearrange("(q s) (ib p) d -> q s p ib d", s=S, p=P)
    adj_v = adj.rearrange("(nb p) w -> nb p w", p=P)
    adj_c = adj.rearrange("(nb p) (wb c) -> wb p nb c", p=P, c=P)

    early = nc.dram_tensor("after_relation", (B, N, D), F32, kind="Internal").ap()
    early_v = early.rearrange("(q s) (ib p) d -> q s p ib d", s=S, p=P)
    mid = nc.dram_tensor("after_attention", (B, N, D), F32, kind="Internal").ap()
    mid_v = mid.rearrange("(q s) (ib p) d -> q s p ib d", s=S, p=P)
    dst_row = nc.dram_tensor("dst_row", (S, N), F32, kind="Internal").ap()
    shift_row = nc.dram_tensor("shift_row", (S, 2, N), F32, kind="Internal").ap()

    def wait(eng, sem, value):
        if not isinstance(value, int) or value > 0:
            eng.wait_ge(sem, value)

    ctx = ExitStack()
    with ctx:
        def sb(name, shape, dt=F32, c=ctx):
            return c.enter_context(nc.sbuf_tensor(name, shape, dt))

        def psum(name, shape, c=ctx):
            return c.enter_context(nc.psum_tensor(name, shape, F32))

        def sem(name, c=ctx):
            return c.enter_context(nc.semaphore(name))

        at_hi = sb("at_hi", [P, NB, N], F32R)
        at_lo = sb("at_lo", [P, NB, N], F32R)
        ident = sb("ident", [P, P])
        eps_t = sb("eps_t", [P, NB])
        half_t = sb("half_t", [P, NB])
        xin = sb("xin", [P, NB, S, D])
        x_in = [sem(f"x_in{s}") for s in range(S)]
        mid_in = sem("mid_in")
        w_all = sb("w_all", [P, K_CONV * D])
        theta_in = sem("theta_in")

        with ExitStack() as c12:
            mask_n = sb("mask_n", [P, NB, N], BF16, c12)
            mask_t = sb("mask_t", [P, NB, N], BF16, c12)
            w0 = sb("w0", [P, D + 2], F32, c12)
            w1 = sb("w1", [P, D + 2], F32, c12)
            w_r = sb("w_r", [P, 1], F32, c12)
            gb = sb("gb", [P, 1], F32, c12)
            g_i = sb("g_i", [P, 1], F32, c12)
            bias0 = sb("bias0", [P, D], F32, c12)
            h_ext = sb("h_ext", [P, S, NB, D + 1], F32, c12)

            with ExitStack() as c:
                a_in = sb("a_in", [P, NB, N], F32, c)
                att_w_t = sb("att_w_t", [P, D], F32, c)
                a_sd = sb("a_sd", [P, 2], F32, c)
                tp = psum("tp", [P, 4, 512], c)
                tw = psum("tw", [P, 512], c)
                td = psum("td", [P, 512], c)
                adj_in = [sem(f"adj_in{n}", c) for n in range(NB)]
                w_in = sem("w_in", c)
                att_in = sem("att_in", c)
                zeroed = sem("zeroed", c)
                made = sem("made", c)
                t_ready = sem("t_ready", c)
                hi_done = sem("hi_done", c)
                lo_done = sem("lo_done", c)
                wt_ready = sem("wt_ready", c)
                wt_done = sem("wt_done", c)
                wsd_ready = sem("wsd_ready", c)
                block = c.enter_context(nc.Block())

                @block.sync
                def _(sp):
                    for n in range(NB):
                        sp.dma_start(a_in[:, n, :], adj_v[n]).then_inc(adj_in[n], 16)
                    for s in range(S):
                        sp.dma_start(xin[:, :, s, :], x_v[0, s]).then_inc(x_in[s], 16)
                    sp.dma_start(w0[:, 0:D], w_rel).then_inc(w_in, 16)
                    col = g_w.rearrange("(n a) -> n a", a=1)
                    sp.dma_start(w0[:, D:D + 1], col[D:2 * D, :]).then_inc(w_in, 16)
                    sp.dma_start(w0[:, D + 1:D + 2], col[0:D, :]).then_inc(w_in, 16)
                    sp.dma_start(w_r[:], g_w[2 * D:2 * D + 1].partition_broadcast(P)).then_inc(w_in, 16)
                    sp.dma_start(gb[:], g_b.rearrange("(a b) -> a b", a=1)[0].partition_broadcast(P)).then_inc(w_in, 16)
                    sp.dma_start(bias0[:], b_rel.partition_broadcast(P)).then_inc(w_in, 16)
                    sp.dma_start(g_i[:], col[D:2 * D, :]).then_inc(w_in, 16)
                    sp.wait_ge(w_in, 16 * 7)

                @block.gpsimd
                def _(pool):
                    pool.memset(ident[:], 0.0).then_inc(zeroed, 1)
                    pool.wait_ge(zeroed, 1)
                    pool.affine_select(out=ident[:], in_=ident[:], compare_op=ALU.not_equal, fill=1.0,
                                       base=0, pattern=[[-1, P]], channel_multiplier=1).then_inc(made, 1)
                    pool.memset(eps_t[:], EPS)
                    pool.memset(half_t[:], -0.5)
                    pool.memset(h_ext[:, :, :, D:D + 1], 1.0)

                @block.tensor
                def _(pe):
                    pe.wait_ge(made, 1)
                    pe.wait_ge(att_in, 64)
                    nc.tensor.transpose(tw[:, 0:P], w1[:, 0:D], ident[:]).then_inc(wt_ready, 1)
                    for h in range(2):
                        for jb in range(NB):
                            u = h * NB + jb
                            if u >= 4:
                                pe.wait_ge(lo_done, u - 3)
                            for k in range(4):
                                ib = h * 4 + k
                                if jb == 0:
                                    pe.wait_ge(adj_in[ib], 16)
                                last = nc.tensor.transpose(tp[:, u % 4, k * P:(k + 1) * P],
                                                           a_in[:, ib, jb * P:(jb + 1) * P], ident[:])
                            last.then_inc(t_ready, 1)
                    pe.wait_ge(wt_done, 1)
                    nc.tensor.matmul(td[:, 0:2], att_w_t[:], a_sd[:], start=True, stop=True).then_inc(wsd_ready, 1)

                @block.scalar
                def _(act):
                    act.dma_start(w1[:, 0:D], w_att).then_inc(att_in, 16)
                    act.dma_start(a_sd[:, 0:1], a_src.rearrange("(n a) -> n a", a=1)).then_inc(att_in, 16)
                    act.dma_start(a_sd[:, 1:2], a_dst.rearrange("(n a) -> n a", a=1)).then_inc(att_in, 16)
                    act.dma_start(w1[:, D:D + 1], a_dst.rearrange("(n a) -> n a", a=1)).then_inc(att_in, 16)
                    act.wait_ge(wt_ready, 1)
                    nc.scalar.activation(att_w_t[:], tw[:, 0:P], ACT.Copy).then_inc(wt_done, 1)
                    for u in range(2 * NB):
                        h, jb = u // NB, u % NB
                        act.wait_ge(t_ready, u + 1)
                        nc.scalar.activation(at_hi[:, jb, h * 512:(h + 1) * 512], tp[:, u % 4, :],
                                             ACT.Copy).then_inc(hi_done, 1)
                    act.wait_ge(wsd_ready, 1)
                    nc.scalar.activation(w1[:, D:D + 2], td[:, 0:2], ACT.Copy)

                @block.vector
                def _(dve):
                    def mask(n):
                        dve.wait_ge(adj_in[n], 16)
                        nc.vector.tensor_scalar(mask_n[:, n, :], a_in[:, n, :], 0.0, FAR, ALU.is_le, ALU.mult)

                    for n in range(NB // 2):
                        mask(n)
                    for u in range(2 * NB):
                        h, jb = u // NB, u % NB
                        if h == 1 and jb % 2 == 0:
                            mask((NB + jb) // 2)
                        half = slice(h * 512, (h + 1) * 512)
                        dve.wait_ge(hi_done, u + 1)
                        nc.vector.tensor_tensor(at_lo[:, jb, half], tp[:, u % 4, :],
                                                at_hi[:, jb, half].bitcast(F32), ALU.subtract).then_inc(lo_done, 1)

            with ExitStack() as c:
                TILES = 4
                x0 = sb("x0", [P, NB, S, D], F32, c)
                x1 = sb("x1", [P, S, NB, D], F32, c)
                x_t = sb("x_t", [P, S, N], F32, c)
                v_f = sb("v_f", [P, NB, S, D], F32, c)
                v_hi = sb("v_hi", [P, NB, S, D], F32R, c)
                v_lo = sb("v_lo", [P, NB, S, D], F32R, c)
                s_j = sb("s_j", [P, NB, S, 1], F32, c)
                x_sum = sb("x_sum", [P, S, 2], F32, c)
                mix = sb("mix", [P, S, D], F32, c)
                row = sb("row", [P, S, D], F32, c)
                stats = sb("stats", [P, S, NB, 6], F32, c)
                stats1 = sb("stats1", [P, S, NB, 6], F32, c)
                means = sb("means", [P, NB], F32, c)
                apart = sb("apart", [P, NB], F32, c)
                apart2 = sb("apart2", [P, NB], F32, c)
                within = sb("within", [P, NB], F32, c)
                within_e = sb("within_e", [P, NB], F32, c)
                dev = sb("dev", [P, NB], F32, c)
                root_dev = sb("root_dev", [P, NB], F32, c)
                m_rs = sb("m_rs", [P, NB], F32, c)
                consts = sb("consts", [P, 4, NB], F32, c)
                rs0 = sb("rs0", [P, S, NB], F32, c)
                rs1 = sb("rs1", [P, S, NB], F32, c)
                nm0 = sb("nm0", [P, S, NB], F32, c)
                nm1 = sb("nm1", [P, S, NB], F32, c)
                e_sd = sb("e_sd", [P, S, NB, 2], F32, c)
                e_d2 = sb("e_d2", [P, S, NB], F32, c)
                e_d8 = sb("e_d8", [P, S, NB], F32, c)
                top = sb("top", [P, S, NB], F32, c)
                z_t = sb("z_t", [P, S, NB], F32, c)
                m_t = sb("m_t", [P, S, NB], F32, c)
                shift = sb("shift", [P, S, 2, NB], F32, c)
                dst_bc = sb("dst_bc", [P, N], F32, c)
                shift_bc = sb("shift_bc", [P, S, 2, N], F32, c)
                pt = sb("pt", [P, TILES, N], F32, c)
                r_den = sb("r_den", [P, NB], F32, c)

                RING = 5
                ring = psum("ring", [P, RING, 512], c)
                att = psum("att", [P, 3, 512], c)
                GROUPS = [(0, 3), (3, 3), (6, 2)]
                LAG = 4

                kinds = ["a"] * 4 + ["d"] * 6 + ["d"] + ["d"] * NB + ["a"] * 5 + ["a"] * 5
                U_T, U_V, U_S, U_Y, U_H = 0, 4, 10, 11, 19
                UNITS = len(kinds)
                SLOTS = UNITS + 1
                assert SLOTS % RING == 0
                REL = {k: kinds.count(k) for k in "ad"}
                order = [kinds[:u + 1].count(kinds[u]) for u in range(UNITS)]

                unit_ready = sem("unit_ready", c)
                freed = {"a": sem("freed_by_scalar", c), "d": sem("freed_by_vector", c)}
                v_hi_done = sem("v_hi_done", c)
                stats0_ready = sem("stats0_ready", c)
                nm0_ready = sem("nm0_ready", c)
                x1_ready = [sem(f"x1_ready{s}", c) for s in range(S)]
                saved = sem("saved", c)
                stored = [sem(f"stored{s}", c) for s in range(S)]
                x1_in = [sem(f"x1_in{s}", c) for s in range(S)]
                dst_out = sem("dst_out", c)
                dst_in = sem("dst_in", c)
                shift_ready = sem("shift_ready", c)
                shift_out = sem("shift_out", c)
                shift_in = [sem(f"shift_in{s}", c) for s in range(S)]
                tile_free = sem("tile_free", c)
                leaky_done = sem("leaky_done", c)
                masked = sem("masked", c)
                exp_done = sem("exp_done", c)
                att_free = sem("att_free", c)
                stats1_ready = sem("stats1_ready", c)
                nm1_ready = sem("nm1_ready", c)
                x2_ready = [sem(f"x2_ready{s}", c) for s in range(S)]
                step = sem("step", c)
                pool_step = sem("pool_step", c)
                block = c.enter_context(nc.Block())

                def v_view(bank, n):
                    return ring[:, bank, 0:n * (D + 2)].rearrange("p (k c) -> p k c", c=D + 2)

                @block.sync
                def _(sp):
                    def dst_to_row(p, s):
                        sp.wait_ge(freed["a"], p * REL["a"] + order[U_H + 5 * s + 4])
                        sp.dma_start(dst_row[s].rearrange("(ib p) -> p ib", p=P), e_sd[:, s, :, 1],
                                     allow_slow_non_contiguous=True).then_inc(dst_out, 16)

                    def spread_dst(p, s):
                        sp.wait_ge(dst_out, p * (16 * S) + (16 * s + 16))
                        sp.dma_start(dst_bc[:], dst_row[s].partition_broadcast(P)).then_inc(dst_in, 16)

                    def shift_to_row(p, s):
                        sp.wait_ge(shift_ready, p * S + (s + 1))
                        for k in range(2):
                            sp.dma_start(shift_row[s, k].rearrange("(ib p) -> p ib", p=P), shift[:, s, k, :],
                                         allow_slow_non_contiguous=True).then_inc(shift_out, 16)

                    def spread_shift(p, s):
                        sp.wait_ge(shift_out, p * (32 * S) + (32 * s + 32))
                        for k in range(2):
                            sp.dma_start(shift_bc[:, s, k, :],
                                         shift_row[s, k].partition_broadcast(P)).then_inc(shift_in[s], 16)

                    def store(p, s):
                        sp.wait_ge(x2_ready[s], p + 1)
                        sp.dma_start(mid_v[p, s], x1[:, s, :, :]).then_inc(stored[s], 16)

                    def save(p):
                        for s in range(S):
                            sp.wait_ge(x1_ready[s], p * 2 + 2)
                            sp.dma_start(early_v[p, s], x0[:, :, s, :]).then_inc(saved, 16)
                        sp.wait_ge(saved, p * (16 * S) + 16 * S)

                    def residual(p, s):
                        wait(sp, stored[s], p * 16)
                        sp.dma_start(x1[:, s, :, :], early_v[p, s]).then_inc(x1_in[s], 16)

                    def reload(p):
                        sp.wait_ge(v_hi_done, (p - 1) * (2 * 3) + 1)
                        for s in range(S):
                            sp.dma_start(xin[:, :, s, :], x_v[p, s]).then_inc(x_in[s], 16)

                    def steady(p, more):
                        if more:
                            reload(p + 2)
                        shift_to_row(p, 1)
                        spread_shift(p, 1)
                        save(p + 1)
                        dst_to_row(p + 1, 0)
                        spread_dst(p + 1, 0)
                        store(p, 0)
                        residual(p + 1, 0)
                        dst_to_row(p + 1, 1)
                        shift_to_row(p + 1, 0)
                        spread_dst(p + 1, 1)
                        spread_shift(p + 1, 0)
                        store(p, 1)
                        residual(p + 1, 1)

                    reload(1)
                    dst_to_row(0, 0)
                    spread_dst(0, 0)
                    save(0)
                    for s in range(S):
                        residual(0, s)
                    dst_to_row(0, 1)
                    shift_to_row(0, 0)
                    spread_dst(0, 1)
                    spread_shift(0, 0)
                    with sp.Fori(0, PAIRS - 2) as p:
                        steady(p, True)
                    steady(PAIRS - 2, False)
                    shift_to_row(PAIRS - 1, 1)
                    spread_shift(PAIRS - 1, 1)
                    sp.dma_start(w_all[:, 0:K_CHEB * D].rearrange("p (k o) -> p k o", o=D),
                                 theta.rearrange("(k f) o -> f k o", f=D)).then_inc(theta_in, 16)
                    for s in range(S):
                        sp.dma_start(xin[:, :, s, :], mid_v[0, s]).then_inc(mid_in, 16)
                    for s in range(S):
                        store(PAIRS - 1, s)
                    for s in range(S):
                        sp.wait_ge(stored[s], 16 * PAIRS)

                @block.tensor
                def _(pe):
                    def bank(p, u):
                        before = u - RING
                        if before < 0:
                            before = before + SLOTS
                            p = p - 1
                        if before == UNITS:
                            before -= RING
                        if not (isinstance(p, int) and p < 0):
                            wait(pe, freed[kinds[before]], p * REL[kinds[before]] + order[before])
                        return u % RING

                    def transposes(p, u, s, src):
                        for half in range(2):
                            if src is x0:
                                pe.wait_ge(x1_ready[s], p * 2 + (half + 1))
                            b = bank(p, u + half)
                            for k in range(4):
                                last = nc.tensor.transpose(ring[:, b, k * P:(k + 1) * P],
                                                           src[:, half * 4 + k, s, :], ident[:])
                            last.then_inc(unit_ready, 1)

                    def project(p, u, u_t, s, w):
                        wait(pe, freed["a"], p * REL["a"] + order[u_t + 1])
                        for g, (b0, n) in enumerate(GROUPS):
                            b = bank(p, u + g)
                            for k in range(n):
                                last = nc.tensor.matmul(v_view(b, n)[:, k, :], x_t[:, s, (b0 + k) * P:(b0 + k + 1) * P],
                                                        w[:], start=True, stop=True)
                            last.then_inc(unit_ready, 1)

                    def relation_head(p):
                        for s in range(S):
                            pe.wait_ge(x_in[s], p * 16 + 16)
                            transposes(p, U_T + 2 * s, s, xin)
                        for s in range(S):
                            project(p, U_V + 3 * s, U_T + 2 * s, s, w0)
                        b = bank(p, U_S)
                        wait(pe, freed["d"], p * REL["d"] + order[U_S - 1])
                        for s in range(S):
                            for half in range(2):
                                nc.tensor.matmul(ring[:, b, s * D:(s + 1) * D],
                                                 x_sum[:, s, half:half + 1].to_broadcast([P, P]), w0[:, 0:D],
                                                 start=(half == 0), stop=(half == 1))
                        for s in range(S):
                            for jb in range(NB):
                                last = nc.tensor.matmul(ring[:, b, (S + s) * D:(S + s + 1) * D],
                                                        s_j[:, jb, s, :].to_broadcast([P, P]), v_f[:, jb, s, :],
                                                        start=(jb == 0), stop=(jb == NB - 1))
                        last.then_inc(unit_ready, 1)

                    def relation_row(p, ib):
                        b = bank(p, U_Y + ib)
                        for jb in range(NB):
                            for n, (a, v) in enumerate(((at_hi, v_hi), (at_hi, v_lo), (at_lo, v_hi))):
                                nc.tensor.matmul(ring[:, b, 0:S * D], a[:, jb, ib * P:(ib + 1) * P],
                                                 v[:, jb, :, :].rearrange("p s d -> p (s d)"),
                                                 start=(jb == 0 and n == 0), stop=False)
                        if ib == 0:
                            pe.wait_ge(freed["d"], p * REL["d"] + order[U_S])
                        for s in range(S):
                            last = nc.tensor.matmul(ring[:, b, s * D:(s + 1) * D], x_t[:, s, ib * P:(ib + 1) * P],
                                                    mix[:, s, :], start=False, stop=(s == S - 1))
                        last.then_inc(unit_ready, 1)

                    def turn(p, s):
                        transposes(p, U_H + 5 * s, s, x0)

                    def heads(p, s):
                        project(p, U_H + 5 * s + 2, U_H + 5 * s, s, w1)

                    def attend(p, s, b0, b1):
                        if b0 == 0:
                            pe.wait_ge(att_free, p * S + (s + 1))
                        for jb in range(b0, b1):
                            pe.wait_ge(exp_done, p * (S * NB) + (s * NB + jb + 1))
                            for g, (g0, n) in enumerate(GROUPS):
                                for k in range(n):
                                    last = nc.tensor.matmul(
                                        att[:, g, k * (D + 1):(k + 1) * (D + 1)],
                                        pt[:, jb % TILES, (g0 + k) * P:(g0 + k + 1) * P], h_ext[:, s, jb, :],
                                        start=(jb == 0 and k == 0), stop=(jb == NB - 1), skip_group_check=True)
                            last.then_inc(tile_free, 1)

                    pe.sem_inc(att_free, 1)
                    pe.sem_inc(tile_free, TILES)
                    relation_head(0)
                    for ib in range(NB):
                        relation_row(0, ib)
                    for s in range(S):
                        turn(0, s)
                        heads(0, s)
                    with pe.Fori(0, PAIRS - 1) as p:
                        relation_head(p + 1)
                        for ib in range(NB):
                            relation_row(p + 1, ib)
                            if ib >= LAG - 1:
                                attend(p, 0, ib - LAG + 1, ib - LAG + 2)
                        attend(p, 0, NB - LAG + 1, NB)
                        turn(p + 1, 0)
                        heads(p + 1, 0)
                        attend(p, 1, 0, NB // 2)
                        turn(p + 1, 1)
                        attend(p, 1, NB // 2, NB)
                        heads(p + 1, 1)
                    for s in range(S):
                        attend(PAIRS - 1, s, 0, NB)

                @block.scalar
                def _(act):
                    def copy_t(p, u, s, total=False):
                        for half in range(2):
                            act.wait_ge(unit_ready, p * UNITS + (u + half + 1))
                            nc.scalar.activation(x_t[:, s, half * 512:(half + 1) * 512], ring[:, (u + half) % RING, :],
                                                 ACT.Copy,
                                                 accum_out=x_sum[:, s, half:half + 1] if total else None
                                                 ).then_inc(freed["a"], 1)

                    def relation(p):
                        for s in range(S):
                            copy_t(p, U_T + 2 * s, s, total=True)
                        for s in range(S):
                            for g, (b0, n) in enumerate(GROUPS):
                                u = U_V + 3 * s + g
                                act.wait_ge(unit_ready, p * UNITS + (u + 1))
                                src = v_view(u % RING, n)[:, :, 0:D]
                                nc.scalar.activation(v_f[:, b0:b0 + n, s, :], src, ACT.Copy)
                                nc.scalar.activation(v_hi[:, b0:b0 + n, s, :], src, ACT.Copy,
                                                     scale=w_r[:, 0:1]).then_inc(v_hi_done, 1)

                    def heads(p, s):
                        u = U_H + 5 * s
                        for g, (b0, n) in enumerate(GROUPS):
                            act.wait_ge(unit_ready, p * UNITS + (u + 2 + g + 1))
                            src = v_view((u + 2 + g) % RING, n)
                            nc.scalar.activation(h_ext[:, s, b0:b0 + n, 0:D], src[:, :, 0:D], ACT.Copy)
                            nc.scalar.activation(e_sd[:, s, b0:b0 + n, :], src[:, :, D:D + 2],
                                                 ACT.Copy).then_inc(freed["a"], 1)

                    def norm0(p, s):
                        act.wait_ge(nm0_ready, p * S + (s + 1))
                        for ib in range(NB):
                            last = nc.scalar.activation(x0[:, ib, s, :], x0[:, ib, s, :], ACT.Identity,
                                                        bias=nm0[:, s, ib:ib + 1], scale=rs0[:, s, ib:ib + 1])
                            if ib % 4 == 3:
                                last.then_inc(x1_ready[s], 1)

                    def norm1(p, s):
                        act.wait_ge(nm1_ready, p * S + (s + 1))
                        for ib in range(NB):
                            last = nc.scalar.activation(x1[:, s, ib, :], x1[:, s, ib, :], ACT.Identity,
                                                        bias=nm1[:, s, ib:ib + 1], scale=rs1[:, s, ib:ib + 1])
                        last.then_inc(x2_ready[s], 1)

                    def expo(p, s, b0, b1):
                        for jb in range(b0, b1):
                            act.wait_ge(masked, p * (S * NB) + (s * NB + jb + 1))
                            nc.scalar.activation(pt[:, jb % TILES, :], pt[:, jb % TILES, :], ACT.Exp,
                                                 bias=e_d2[:, s, jb:jb + 1]).then_inc(exp_done, 1)

                    def steady(p, more):
                        expo(p, 0, 0, NB)
                        norm0(p + 1, 0)
                        copy_t(p + 1, U_H, 0)
                        expo(p, 1, 0, 1)
                        heads(p + 1, 0)
                        expo(p, 1, 1, 2)
                        norm0(p + 1, 1)
                        expo(p, 1, 2, 4)
                        norm1(p, 0)
                        copy_t(p + 1, U_H + 5, 1)
                        expo(p, 1, 4, NB)
                        heads(p + 1, 1)
                        if more:
                            relation(p + 2)
                        norm1(p, 1)

                    relation(0)
                    for s in range(S):
                        norm0(0, s)
                        copy_t(0, U_H + 5 * s, s)
                        heads(0, s)
                    relation(1)
                    with act.Fori(0, PAIRS - 2) as p:
                        steady(p, True)
                    steady(PAIRS - 2, False)
                    expo(PAIRS - 1, 0, 0, NB)
                    expo(PAIRS - 1, 1, 0, NB)
                    for s in range(S):
                        norm1(PAIRS - 1, s)

                @block.vector
                def _(dve):
                    count = [0]

                    def link(ins):
                        count[0] += 1
                        ins.then_inc(step, 1)
                        dve.wait_ge(step, count[0])

                    def restart():
                        dve.sem_clear(step)
                        count[0] = 0

                    def project(p):
                        for s in range(S):
                            for g, (b0, n) in enumerate(GROUPS):
                                u = U_V + 3 * s + g
                                src = v_view(u % RING, n)
                                dve.wait_ge(v_hi_done, p * (2 * 3) + (s * 3 + g + 1))
                                nc.vector.scalar_tensor_tensor(
                                    out=v_lo[:, b0:b0 + n, s, :], in0=src[:, :, 0:D], scalar=w_r[:, 0:1],
                                    in1=v_hi[:, b0:b0 + n, s, :].bitcast(F32), op0=ALU.mult, op1=ALU.subtract)
                                nc.vector.tensor_copy(s_j[:, b0:b0 + n, s, :], src[:, :, D + 1:D + 2]).then_inc(freed["d"], 1)

                    def sums(p):
                        dve.wait_ge(unit_ready, p * UNITS + (U_S + 1))
                        src = ring[:, U_S % RING, :].rearrange("p (k s d) -> p k s d", k=2, s=S)
                        for t in range(S):
                            nc.vector.scalar_tensor_tensor(out=mix[:, t, :], in0=src[:, 0, t, :], scalar=g_i[:, 0:1],
                                                           in1=ident[:], op0=ALU.mult, op1=ALU.add)
                        link(nc.vector.tensor_tensor(row[:], src[:, 1, :, :],
                                                     bias0[:].unsqueeze(1).broadcast_to([P, S, D]), ALU.add))
                        nc.vector.scalar_tensor_tensor(out=row[:], in0=src[:, 0, :, :], scalar=gb[:, 0:1],
                                                       in1=row[:], op0=ALU.mult, op1=ALU.add).then_inc(freed["d"], 1)
                        dve.wait_ge(freed["d"], p * REL["d"] + order[U_S])

                    def row_sum(p, ib):
                        u = U_Y + ib
                        if ib == 0:
                            wait(dve, saved, p * (16 * S))
                        dve.wait_ge(unit_ready, p * UNITS + (u + 1))
                        nc.vector.tensor_tensor(x0[:, ib, :, :], ring[:, u % RING, 0:S * D].rearrange("p (s d) -> p s d", s=S),
                                                row[:], ALU.add).then_inc(freed["d"], 1)

                    def row_stats(p, ib):
                        dve.wait_ge(freed["d"], p * REL["d"] + order[U_Y + ib])
                        for s in range(S):
                            last = nc.vector.bn_stats(stats[:, s, ib, :], x0[:, ib, s, :])
                        if ib == NB - 1:
                            last.then_inc(stats0_ready, 1)

                    def maximum(p, s):
                        dve.wait_ge(dst_in, p * (16 * S) + (16 * s + 16))
                        nc.vector.tensor_scalar(e_d2[:, s, :], e_sd[:, s, :, 1], SLOPE, None, ALU.mult)
                        nc.vector.tensor_scalar(e_d8[:, s, :], e_sd[:, s, :, 1], 1.0 - SLOPE, None, ALU.mult)
                        for ib in range(NB):
                            unwanted = shift_bc[:, 1, ib % 2, 0:N // 2].bitcast(BF16)
                            count[0] += 1
                            nc.vector.tensor_tensor_reduce(unwanted, mask_n[:, ib, :], dst_bc[:], 1.0,
                                                           3 * FAR, ALU.add, ALU.max,
                                                           top[:, s, ib:ib + 1]).then_inc(step, 1)
                            dve.wait_ge(step, count[0] - (1 if ib < NB - 1 else 0))
                        src = e_sd[:, s, :, 0]
                        link(nc.vector.tensor_tensor(z_t[:, s, :], src, top[:, s, :], ALU.add))
                        link(nc.vector.scalar_tensor_tensor(out=m_t[:, s, :], in0=z_t[:, s, :], scalar=SLOPE,
                                                            in1=z_t[:, s, :], op0=ALU.mult, op1=ALU.max))
                        nc.vector.tensor_tensor(shift[:, s, 0, :], src, m_t[:, s, :], ALU.subtract)
                        nc.vector.scalar_tensor_tensor(out=shift[:, s, 1, :], in0=src, scalar=SLOPE, in1=m_t[:, s, :],
                                                       op0=ALU.mult, op1=ALU.subtract).then_inc(shift_ready, 1)

                    def leaky(p, s, jb):
                        if jb == 0:
                            dve.wait_ge(shift_in[s], p * 32 + 32)
                        dve.wait_ge(tile_free, p * (S * NB) + (s * NB + jb + 1))
                        nc.vector.scalar_tensor_tensor(out=pt[:, jb % TILES, :], in0=shift_bc[:, s, 0, :],
                                                       scalar=e_d8[:, s, jb:jb + 1], in1=shift_bc[:, s, 1, :],
                                                       op0=ALU.add, op1=ALU.max).then_inc(leaky_done, 1)

                    def mask(p, s, jb):
                        tile = pt[:, jb % TILES, :]
                        dve.wait_ge(leaky_done, p * (S * NB) + (s * NB + jb + 1))
                        nc.vector.tensor_tensor(tile, tile, mask_t[:, jb, :], ALU.add).then_inc(masked, 1)

                    def scores(p, s, b0, b1):
                        for jb in range(b0, b1 + 1):
                            if jb < b1:
                                leaky(p, s, jb)
                            if jb > b0:
                                mask(p, s, jb - 1)

                    def finish(p, s):
                        dve.wait_ge(tile_free, p * (S * NB) + (s * NB + NB + TILES))
                        dve.wait_ge(x1_in[s], p * 16 + 16)
                        for g, (b0, n) in enumerate(GROUPS):
                            src = att[:, g, 0:n * (D + 1)].rearrange("p (k c) -> p k c", c=D + 1)
                            last = nc.vector.reciprocal(r_den[:, b0:b0 + n], src[:, :, D])
                        link(last)
                        for g, (b0, n) in enumerate(GROUPS):
                            for k in range(n):
                                last = nc.vector.scalar_tensor_tensor(
                                    out=x1[:, s, b0 + k, :], in0=att[:, g, k * (D + 1):k * (D + 1) + D],
                                    scalar=r_den[:, b0 + k:b0 + k + 1], in1=x1[:, s, b0 + k, :], op0=ALU.mult, op1=ALU.add)
                        last.then_inc(att_free, 1)
                        dve.wait_ge(att_free, p * S + (s + 2))
                        for ib in range(NB):
                            last = nc.vector.bn_stats(stats1[:, s, ib, :], x1[:, s, ib, :])
                        last.then_inc(stats1_ready, 1)

                    project(0)
                    sums(0)
                    for ib in range(NB):
                        row_sum(0, ib)
                        row_stats(0, ib)
                    for jb in range(NB):
                        nc.vector.tensor_scalar(mask_t[:, jb, :], at_hi[:, jb, :].bitcast(F32), 0.0, FAR,
                                                ALU.is_le, ALU.mult)
                    maximum(0, 0)
                    project(1)
                    restart()

                    def steady(p, more):
                        scores(p, 0, 0, 1)
                        sums(p + 1)
                        scores(p, 0, 1, 2)
                        maximum(p, 1)
                        for n in range(NB // 2):
                            leaky(p, 0, n + 2)
                            row_sum(p + 1, 2 * n)
                            mask(p, 0, n + 2)
                            row_stats(p + 1, 2 * n)
                            if n == NB // 2 - 1:
                                scores(p, 0, 6, 7)
                            row_sum(p + 1, 2 * n + 1)
                            row_stats(p + 1, 2 * n + 1)
                        scores(p, 0, 7, NB)
                        scores(p, 1, 0, 2)
                        finish(p, 0)
                        scores(p, 1, 2, NB)
                        maximum(p + 1, 0)
                        if more:
                            project(p + 2)
                        finish(p, 1)
                        restart()

                    with dve.Fori(0, PAIRS - 2) as p:
                        steady(p, True)
                    steady(PAIRS - 2, False)
                    scores(PAIRS - 1, 0, 0, 2)
                    maximum(PAIRS - 1, 1)
                    scores(PAIRS - 1, 0, 2, NB)
                    scores(PAIRS - 1, 1, 0, 2)
                    finish(PAIRS - 1, 0)
                    scores(PAIRS - 1, 1, 2, NB)
                    finish(PAIRS - 1, 1)

                @block.gpsimd
                def _(pool):
                    def link(ins):
                        ins.then_inc(pool_step, 1)
                        pool.wait_ge(pool_step, 1)
                        pool.sem_clear(pool_step)

                    def root(st, rs, nm, done):
                        tt = pool.tensor_tensor
                        tt(apart[:], st[:, :, 1], st[:, :, 4], ALU.subtract)
                        tt(within[:], st[:, :, 2], st[:, :, 5], ALU.add)
                        link(tt(means[:], st[:, :, 1], st[:, :, 4], ALU.add))
                        tt(within_e[:], within[:], consts[:, 1, :], ALU.add)
                        link(tt(apart2[:], apart[:], apart[:], ALU.mult))
                        link(tt(apart[:], apart2[:], consts[:, 0, :], ALU.mult))
                        link(tt(dev[:], within_e[:], apart[:], ALU.add))
                        link(tt(root_dev[:], dev[:], half_t[:, 0:NB], ALU.pow))
                        tt(rs, root_dev[:], consts[:, 2, :], ALU.mult)
                        link(tt(m_rs[:], means[:], root_dev[:], ALU.mult))
                        tt(nm, m_rs[:], consts[:, 3, :], ALU.mult).then_inc(done, 1)

                    def relation(p):
                        pool.wait_ge(stats0_ready, p + 1)
                        for s in range(S):
                            root(stats[:, s, :, :], rs0[:, s, :], nm0[:, s, :], nm0_ready)

                    def finish(p, s):
                        pool.wait_ge(stats1_ready, p * S + (s + 1))
                        root(stats1[:, s, :, :], rs1[:, s, :], nm1[:, s, :], nm1_ready)

                    for n, value in enumerate((D / 4, D * EPS, D ** 0.5, -D ** 0.5 / 2)):
                        last = pool.memset(consts[:, n, :], value)
                    link(last)
                    relation(0)
                    with pool.Fori(0, PAIRS - 1) as p:
                        relation(p + 1)
                        for s in range(S):
                            finish(p, s)
                    for s in range(S):
                        finish(PAIRS - 1, s)

        with ExitStack() as c:
            a_hi = sb("a_hi", [P, NB, N], F32R, c)
            a_lo = sb("a_lo", [P, NB, N], F32R, c)
            STAGE = 3
            a_in = sb("a_part", [P, STAGE, NB, P], F32, c)
            xb = sb("xb", [P, NB, S, D], F32, c)
            x_t = sb("x_t3", [P, NB, S, D], F32, c)
            z_hi = sb("z_hi", [P, 2, NB, S, D], F32R, c)
            z_lo = sb("z_lo", [P, 2, NB, S, D], F32R, c)
            y_t = sb("y_t3", [P, S, D], F32, c)
            w2 = sb("w2", [P, 3, D], F32, c)
            w3 = sb("w3", [P, 4, D], F32, c)
            bias2 = sb("bias2", [P, S, D], F32, c)
            stats = sb("stats3", [P, 2, S, 6], F32, c)
            mv = sb("mv3", [P, 2, S, 2], F32, c)
            var_e = sb("var_e3", [P, 2, S], F32, c)
            rs = sb("rs3", [P, 2, S], F32, c)
            RING = 8
            ring = psum("ring3", [P, RING, 512], c)

            HOPS = (2, 3)
            kinds, base = [], []
            for hops in HOPS:
                base.append(len(kinds))
                kinds += ["a"] * (NB // 2) + ["d"] * (NB * (1 + hops))
            UNITS = len(kinds)
            assert UNITS % RING == 0
            REL = {k: kinds.count(k) for k in "ad"}
            order = [kinds[:u + 1].count(kinds[u]) for u in range(UNITS)]
            SPLITS = NB * sum(HOPS)

            adj_in = [sem(f"adj_part{n}", c) for n in range(STAGE)]
            a_hi_done = sem("a_hi_done", c)
            a_lo_done = sem("a_lo_done", c)
            conv_in = sem("conv_in", c)
            w2_ready = sem("w2_ready", c)
            w3_ready = sem("w3_ready", c)
            bias_in = sem("bias_in", c)
            copied = sem("copied", c)
            unit_ready = sem("unit_ready3", c)
            freed = {"a": sem("freed_by_scalar3", c), "d": sem("freed_by_vector3", c)}
            split_hi = sem("split_hi", c)
            mv_ready = sem("mv_ready3", c)
            rs_ready = sem("rs_ready3", c)
            normed = sem("normed", c)
            stored = sem("stored3", c)
            step = sem("step3", c)
            pool_step = sem("pool_step3", c)
            block = c.enter_context(nc.Block())
            BLOCKS = len(HOPS) * NB

            @block.sync
            def _(sp):
                def load_x(q):
                    for s in range(S):
                        sp.dma_start(xin[:, :, s, :], mid_v[q, s]).then_inc(mid_in, 16)

                def store(q, b0=0, b1=NB):
                    sp.wait_ge(normed, q * BLOCKS + (BLOCKS - NB + b1))
                    for s in range(S):
                        sp.dma_start(out_v[q, s][:, b0:b1, :], xb[:, b0:b1, s, :]).then_inc(stored, 16)

                for s in range(S):
                    sp.dma_start(bias2[:, s, :], b_cheb.partition_broadcast(P)).then_inc(bias_in, 16)
                for n in range(NB):
                    if n >= STAGE:
                        sp.wait_ge(a_lo_done, n - STAGE + 1)
                    sp.dma_start(a_in[:, n % STAGE, :, :], adj_c[n]).then_inc(adj_in[n % STAGE], 16)
                with sp.Fori(0, PAIRS - 1) as q:
                    sp.wait_ge(copied, q + 1)
                    load_x(q + 1)
                    store(q)
                store(PAIRS - 1, 0, NB - 2)
                store(PAIRS - 1, NB - 2, NB)
                sp.wait_ge(stored, 16 * S * (PAIRS + 1))

            @block.tensor
            def _(pe):
                def bank(q, u):
                    before = u - RING
                    if before < 0:
                        before, q = before + UNITS, q - 1
                    if not (isinstance(q, int) and q < 0):
                        wait(pe, freed[kinds[before]], q * REL[kinds[before]] + order[before])
                    return u % RING

                def times_w(q, b, ib, w, start):
                    for s in range(S):
                        last = nc.tensor.matmul(ring[:, b, s * D:(s + 1) * D], x_t[:, ib, s, :], w,
                                                start=start, stop=(start or s == S - 1))
                    return last

                def layer(q, n, src, a_h, a_l, w):
                    u = base[n]

                    def transposes(t):
                        if n == 0 and t == 0:
                            pe.wait_ge(mid_in, q * (16 * S) + 16 * S)
                        if n == 1:
                            pe.wait_ge(normed, q * BLOCKS + (2 * t + 2))
                        b = bank(q, u + t)
                        for k in range(2):
                            for s in range(S):
                                last = nc.tensor.transpose(ring[:, b, (k * S + s) * P:(k * S + s + 1) * P],
                                                           src[:, 2 * t + k, s, :], ident[:])
                        last.then_inc(unit_ready, 1)

                    for t in range(NB // 2):
                        transposes(t)
                    u += NB // 2
                    if isinstance(q, int) and q == 0:
                        pe.wait_ge((w2_ready, w3_ready)[n], 1)
                    for ib in range(NB):
                        if ib % 2 == 0:
                            wait(pe, freed["a"], q * REL["a"] + order[base[n] + ib // 2])
                        b = bank(q, u + ib)
                        times_w(q, b, ib, w[:, 0, :], True).then_inc(unit_ready, 1)
                    for hop in range(HOPS[n]):
                        u += NB
                        for ib in range(NB):
                            if isinstance(q, int) and q == 0 and n == 0 and hop == 0:
                                pe.wait_ge(a_lo_done, ib + 1)
                            b = bank(q, u + ib)
                            for jb in range(NB):
                                if ib == 0:
                                    wait(pe, freed["d"], q * REL["d"] + order[u - NB + jb])
                                for k, (a, z) in enumerate(((a_h, z_hi), (a_h, z_lo), (a_l, z_hi))):
                                    nc.tensor.matmul(ring[:, b, 0:S * D], a[:, jb, ib * P:(ib + 1) * P],
                                                     z[:, hop % 2, jb, :, :].rearrange("p s d -> p (s d)"),
                                                     start=(jb == 0 and k == 0), stop=False)
                            times_w(q, b, ib, w[:, hop + 1, :], False).then_inc(unit_ready, 1)

                def pair(q):
                    layer(q, 0, xin, a_hi, a_lo, w2)
                    layer(q, 1, xb, at_hi, at_lo, w3)

                pair(0)
                with pe.Fori(1, PAIRS) as q:
                    pair(q)

            @block.scalar
            def _(act):
                def split_graph(i):
                    act.wait_ge(adj_in[i % STAGE], 16 * (i // STAGE + 1))
                    nc.scalar.activation(a_hi[:, :, i * P:(i + 1) * P], a_in[:, i % STAGE, :, :],
                                         ACT.Copy).then_inc(a_hi_done, 1)

                def layer(q, n):
                    u = base[n]
                    for t in range(NB // 2):
                        act.wait_ge(unit_ready, q * UNITS + (u + t + 1))
                        nc.scalar.activation(x_t[:, 2 * t:2 * t + 2, :, :].rearrange("p k s d -> p (k s d)"),
                                             ring[:, (u + t) % RING, :], ACT.Copy).then_inc(freed["a"], 1)
                    u += NB // 2
                    for k in range(HOPS[n]):
                        opening = isinstance(q, int) and q == 0 and n == 0 and k == 0
                        for ib in range(NB):
                            if opening and ib == NB // 2:
                                split_graph(0)
                            act.wait_ge(unit_ready, q * UNITS + (u + ib + 1))
                            nc.scalar.activation(z_hi[:, k % 2, ib, :, :].rearrange("p s d -> p (s d)"),
                                                 ring[:, (u + ib) % RING, 0:S * D], ACT.Copy).then_inc(split_hi, 1)
                        u += NB
                        if opening:
                            for i in range(1, NB):
                                split_graph(i)
                        if n == 0 and k == 0:
                            wait(act, stored, q * (16 * S))
                            nc.scalar.activation(xb[:], xin[:], ACT.Copy).then_inc(copied, 1)

                def pair(q):
                    layer(q, 0)
                    layer(q, 1)

                act.wait_ge(w2_ready, 1)
                act.dma_start(w_all[:], w_conv.rearrange("i o k -> i (o k)")).then_inc(conv_in, 16)
                pair(0)
                with act.Fori(1, PAIRS) as q:
                    pair(q)

            @block.vector
            def _(dve):
                count = [0]

                def link(ins):
                    count[0] += 1
                    ins.then_inc(step, 1)
                    dve.wait_ge(step, count[0])

                def weights():
                    dve.wait_ge(theta_in, 16)
                    th = w_all[:, 0:K_CHEB * D].rearrange("p (k o) -> p k o", o=D)
                    nc.vector.tensor_tensor(w2[:, 1, :], th[:, 1, :], th[:, 3, :], ALU.add)
                    link(nc.vector.tensor_tensor(w2[:, 0, :], th[:, 2, :], th[:, 4, :], ALU.add))
                    link(nc.vector.tensor_tensor(w2[:, 2, :], th[:, 0, :], w2[:, 0, :], ALU.subtract))
                    nc.vector.tensor_scalar(w2[:, 0, :], w2[:, 0, :], 2.0, None, ALU.mult).then_inc(w2_ready, 1)
                    dve.wait_ge(conv_in, 16)
                    cv = w_all[:].rearrange("p (o k) -> p k o", k=K_CONV)
                    nc.vector.tensor_copy(w3[:, 3, :], cv[:, 0, :])
                    for k in range(3):
                        last = nc.vector.tensor_tensor(w3[:, 2 - k, :], cv[:, 1 + k, :], cv[:, 4 + k, :], ALU.add)
                    last.then_inc(w3_ready, 1)

                def stats_of(ib):
                    for s in range(S):
                        last = nc.vector.bn_stats(stats[:, ib % 2, s, :], xb[:, ib, s, :])
                    link(last)
                    for s in range(S):
                        last = nc.vector.bn_aggr(mv[:, ib % 2, s, :], stats[:, ib % 2, s, :])
                    last.then_inc(mv_ready, 1)

                def norm(q, n, ib):
                    dve.wait_ge(rs_ready, q * BLOCKS + (n * NB + ib + 1))
                    for s in range(S):
                        last = nc.vector.tensor_scalar(xb[:, ib, s, :], xb[:, ib, s, :], mv[:, ib % 2, s, 0:1],
                                                       rs[:, ib % 2, s:s + 1], ALU.subtract, ALU.mult)
                    last.then_inc(normed, 1)

                def split_graph(i):
                    dve.wait_ge(a_hi_done, i + 1)
                    nc.vector.tensor_tensor(a_lo[:, :, i * P:(i + 1) * P], a_in[:, i % STAGE, :, :],
                                            a_hi[:, :, i * P:(i + 1) * P].bitcast(F32),
                                            ALU.subtract).then_inc(a_lo_done, 1)

                def layer(q, n):
                    u = base[n] + NB // 2
                    done = NB * sum(HOPS[:n])
                    for k in range(HOPS[n]):
                        opening = isinstance(q, int) and q == 0 and n == 0 and k == 0
                        for ib in range(NB):
                            if opening and ib == NB // 2:
                                split_graph(0)
                            dve.wait_ge(split_hi, q * SPLITS + (done + k * NB + ib + 1))
                            nc.vector.tensor_tensor(z_lo[:, k % 2, ib, :, :].rearrange("p s d -> p (s d)"),
                                                    ring[:, (u + ib) % RING, 0:S * D],
                                                    z_hi[:, k % 2, ib, :, :].rearrange("p s d -> p (s d)").bitcast(F32),
                                                    ALU.subtract).then_inc(freed["d"], 1)
                        u += NB
                        if opening:
                            for i in range(1, NB):
                                split_graph(i)
                    for ib in range(NB):
                        if n == 0 and ib == 0:
                            dve.wait_ge(copied, q + 1)
                        dve.wait_ge(unit_ready, q * UNITS + (u + ib + 1))
                        got = ring[:, (u + ib) % RING, 0:S * D].rearrange("p (s d) -> p s d", s=S)
                        if n == 0:
                            nc.vector.tensor_tensor(y_t[:], got, bias2[:], ALU.add).then_inc(freed["d"], 1)
                            dve.wait_ge(freed["d"], q * REL["d"] + order[u + ib])
                            link(nc.vector.scalar_tensor_tensor(out=xb[:, ib, :, :].rearrange("p s d -> p (s d)"),
                                                                in0=y_t[:].rearrange("p s d -> p (s d)"), scalar=0.0,
                                                                in1=xb[:, ib, :, :].rearrange("p s d -> p (s d)"),
                                                                op0=ALU.max, op1=ALU.add))
                        else:
                            nc.vector.tensor_tensor(xb[:, ib, :, :], got, xb[:, ib, :, :], ALU.add).then_inc(freed["d"], 1)
                            dve.wait_ge(freed["d"], q * REL["d"] + order[u + ib])
                        stats_of(ib)
                        if ib > 0:
                            norm(q, n, ib - 1)
                    norm(q, n, NB - 1)

                def pair(q):
                    layer(q, 0)
                    layer(q, 1)
                    dve.sem_clear(step)
                    count[0] = 0

                weights()
                dve.wait_ge(bias_in, 16 * S)
                pair(0)
                with dve.Fori(1, PAIRS) as q:
                    pair(q)

            @block.gpsimd
            def _(pool):
                def roots(q):
                    for n in range(BLOCKS):
                        k = n % 2
                        pool.wait_ge(mv_ready, q * BLOCKS + (n + 1))
                        pool.tensor_tensor(var_e[:, k, :], mv[:, k, :, 1], eps_t[:, 0:S], ALU.add).then_inc(pool_step, 1)
                        pool.wait_ge(pool_step, 1)
                        pool.sem_clear(pool_step)
                        pool.tensor_tensor(rs[:, k, :], var_e[:, k, :], half_t[:, 0:S], ALU.pow).then_inc(rs_ready, 1)

                with pool.Fori(0, PAIRS) as q:
                    roots(q)


_INS = ['x', 'adj', 'L0_gnn_g_w', 'L0_gnn_g_b', 'L0_gnn_weight', 'L0_gnn_bias', 'L1_gnn_w', 'L1_gnn_a_src',
        'L1_gnn_a_dst', 'L2_gnn_Theta1', 'L2_gnn_bias', 'L3_gnn_weight_1']
_OUTS = [((8, 1024, 128), 'float32')]


def kernel(**inputs):
    import numpy as _np
    import concourse.bacc as _bacc
    from concourse import mybir as _mybir
    from concourse.bass_utils import run_bass_kernel_spmd as _run

    nc = _bacc.Bacc("TRN2", target_bir_lowering=False, num_devices=1)
    arrays, args = {}, []
    for name in _INS:
        a = _np.ascontiguousarray(inputs[name]).reshape(_np.shape(inputs[name]) or (1,))
        arrays[f"in_{name}_dram"] = a
        args.append(nc.dram_tensor(f"in_{name}_dram", a.shape, _mybir.dt.from_np(a.dtype), kind="ExternalInput").ap())
    for i, (shape, dtype) in enumerate(_OUTS):
        dt = _mybir.dt.from_np(_np.dtype(dtype))
        args.append(nc.dram_tensor(f"out_{i}_dram", shape, dt, kind="ExternalOutput").ap())
    gnn_kernel(nc, *args)
    r = _run(nc, [arrays], core_ids=[0])
    got = tuple(r.results[0][f"out_{i}_dram"] for i in range(len(_OUTS)))
    return got[0]
```
